# Optimizing a Trainium2 kernel written in Bass

```python
import numpy as np
import jax
import jax.numpy as jnp

def _softmax(x, axis=-1):
    return jax.nn.softmax(x, axis=axis)

def _gelu(x):
    return jax.nn.gelu(x, approximate=True)

def _silu(x):
    return jax.nn.silu(x)

def _sigmoid(x):
    return jax.nn.sigmoid(x)

def _layernorm(x, axis=-1, eps=1e-05):
    m = jnp.mean(x, axis=axis, keepdims=True)
    v = jnp.var(x, axis=axis, keepdims=True)
    return (x - m) / jnp.sqrt(v + eps)

def _scatter_add(tgt, idx, src, axis=0):
    return tgt.at[idx].add(src)

def _segment_sum(src, seg, n):
    return jax.ops.segment_sum(src, seg, n)
kernel_name = 'mk_seq_preln_d2_jaxref_r8_ee6dfa'

def setup_inputs(seed: int=0):
    np.random.seed(seed)
    _w = jnp.asarray

    def _L0_attn_setup():
        import jax, jax.numpy as jnp
        import numpy as np
        EMB = 256
        HEADS = 16
        G = 2
        HEAD_DIM = EMB // HEADS
        KV = HEADS // G
        B = 2
        S = 256

        def compute_rope(x):
            D = x.shape[2]
            half = D // 2
            inv_freq = 1.0 / 10000.0 ** (jnp.arange(0, half, dtype=jnp.float32) * 2.0 / D)
            pos = jnp.arange(x.shape[1], dtype=jnp.float32)
            ang = pos[:, None] * inv_freq[None, :]
            cos = jnp.concatenate([jnp.cos(ang), jnp.cos(ang)], axis=-1)[None, :, :, None]
            sin = jnp.concatenate([jnp.sin(ang), jnp.sin(ang)], axis=-1)[None, :, :, None]
            x1, x2 = (x[:, :, :half], x[:, :, half:])
            rot = jnp.concatenate([-x2, x1], axis=2)
            return x * cos + rot * sin
        key = jax.random.key(seed)
        ks = jax.random.split(key, 5)
        sc = 0.02
        return {'x': jax.random.normal(ks[0], (B, S, EMB), dtype=jnp.float32), 'W_Q': jax.random.normal(ks[1], (EMB, EMB), dtype=jnp.float32) * sc, 'W_K': jax.random.normal(ks[2], (EMB // G, EMB), dtype=jnp.float32) * sc, 'W_V': jax.random.normal(ks[3], (EMB // G, EMB), dtype=jnp.float32) * sc, 'W_O': jax.random.normal(ks[4], (EMB, EMB), dtype=jnp.float32) * sc}
    _L0_attn_in = _L0_attn_setup()

    def _L0_ffn_setup():
        import jax, jax.numpy as jnp
        import numpy as np
        E = 8
        K = 2
        DIM = 256
        INTER = 176
        N_SHARED = 2
        STD = 0.02
        key = jax.random.key(seed)
        ks = jax.random.split(key, 9)
        B, S = (2, 256)
        return {'x': jax.random.normal(ks[0], (B, S, DIM), dtype=jnp.float32), 'gate_w': jax.random.normal(ks[1], (E, DIM), dtype=jnp.float32) * STD, 'router_bias': jnp.zeros((E,), dtype=jnp.float32), 'W1': jax.random.normal(ks[2], (E, DIM, INTER), dtype=jnp.float32) * STD, 'W3': jax.random.normal(ks[3], (E, DIM, INTER), dtype=jnp.float32) * STD, 'W2': jax.random.normal(ks[4], (E, INTER, DIM), dtype=jnp.float32) * STD, 'sw1': jax.random.normal(ks[5], (N_SHARED * INTER, DIM), dtype=jnp.float32) * STD, 'sw3': jax.random.normal(ks[6], (N_SHARED * INTER, DIM), dtype=jnp.float32) * STD, 'sw2': jax.random.normal(ks[7], (DIM, N_SHARED * INTER), dtype=jnp.float32) * STD}
    _L0_ffn_in = _L0_ffn_setup()

    def _L1_attn_setup():
        import jax, jax.numpy as jnp
        import numpy as np
        ROPE_THETA = 10000.0

        def rope(t, rot_dim):
            S = t.shape[-2]
            half = rot_dim // 2
            inv_freq = 1.0 / ROPE_THETA ** (jnp.arange(0, rot_dim, 2, dtype=jnp.float32) / rot_dim)
            freqs = jnp.arange(S, dtype=jnp.float32)[:, None] * inv_freq[None, :]
            freqs = jnp.repeat(freqs, 2, axis=-1)
            cos, sin = (jnp.cos(freqs), jnp.sin(freqs))
            t_rot, t_pass = (t[..., :rot_dim], t[..., rot_dim:])
            x = t_rot.reshape(*t_rot.shape[:-1], half, 2)
            rh = jnp.stack([-x[..., 1], x[..., 0]], axis=-1).reshape(t_rot.shape)
            t_rot = t_rot * cos + rh * sin
            return jnp.concatenate([t_rot, t_pass], axis=-1)

        def feature_map(x):
            norm = jnp.sqrt(jnp.sum(x * x, axis=-1, keepdims=True))
            return x / jnp.maximum(norm, 1e-12)
        key = jax.random.key(seed)
        kx, kwi, kwo = jax.random.split(key, 3)
        B, S, D = (8, 512, 256)
        scale = 0.02
        return {'X': jax.random.normal(kx, (B, S, D), dtype=jnp.float32), 'W_in': jax.random.normal(kwi, (3 * D, D), dtype=jnp.float32) * scale, 'b_in': jnp.zeros((3 * D,), dtype=jnp.float32), 'W_out': jax.random.normal(kwo, (D, D), dtype=jnp.float32) * scale, 'b_out': jnp.zeros((D,), dtype=jnp.float32)}
    _L1_attn_in = _L1_attn_setup()

    def _L1_ffn_setup():
        import jax, jax.numpy as jnp
        import numpy as np
        EPS = 1e-08

        def _quantize(w):
            gamma = jnp.mean(jnp.abs(w))
            return jnp.clip(jnp.round(w / (gamma + EPS)), -1.0, 1.0)

        def _bitlinear(x, w):
            return jnp.matmul(x, _quantize(w).T)
        key = jax.random.key(seed)
        k1, k2, k3, k4 = jax.random.split(key, 4)
        d, h = (256, 704)
        x = jax.random.normal(k1, (4, 256, d), dtype=jnp.float32)
        w1 = jax.random.normal(k2, (h, d), dtype=jnp.float32)
        w2 = jax.random.normal(k3, (h, d), dtype=jnp.float32)
        w3 = jax.random.normal(k4, (d, h), dtype=jnp.float32)
        return {'x': x, 'w1': w1, 'w2': w2, 'w3': w3}
    _L1_ffn_in = _L1_ffn_setup()
    _d = {'L0_attn_x': _L0_attn_in['x'], 'L0_attn_W_Q': _L0_attn_in['W_Q'], 'L0_attn_W_K': _L0_attn_in['W_K'], 'L0_attn_W_V': _L0_attn_in['W_V'], 'L0_attn_W_O': _L0_attn_in['W_O'], 'L0_ffn_gate_w': _L0_ffn_in['gate_w'], 'L0_ffn_router_bias': _L0_ffn_in['router_bias'], 'L0_ffn_W1': _L0_ffn_in['W1'], 'L0_ffn_W3': _L0_ffn_in['W3'], 'L0_ffn_W2': _L0_ffn_in['W2'], 'L0_ffn_sw1': _L0_ffn_in['sw1'], 'L0_ffn_sw3': _L0_ffn_in['sw3'], 'L0_ffn_sw2': _L0_ffn_in['sw2'], 'L1_attn_W_in': _L1_attn_in['W_in'], 'L1_attn_b_in': _L1_attn_in['b_in'], 'L1_attn_W_out': _L1_attn_in['W_out'], 'L1_attn_b_out': _L1_attn_in['b_out'], 'L1_ffn_w1': _L1_ffn_in['w1'], 'L1_ffn_w2': _L1_ffn_in['w2'], 'L1_ffn_w3': _L1_ffn_in['w3']}
    _x0 = _d['L0_attn_x']
    _d['L0_attn_x'] = jax.random.normal(jax.random.fold_in(jax.random.key(seed), 1), (8, 256, 256), dtype=_x0.dtype)
    del _x0
    return _d

def reference(L0_attn_x, L0_attn_W_Q, L0_attn_W_K, L0_attn_W_V, L0_attn_W_O, L0_ffn_gate_w, L0_ffn_router_bias, L0_ffn_W1, L0_ffn_W3, L0_ffn_W2, L0_ffn_sw1, L0_ffn_sw3, L0_ffn_sw2, L1_attn_W_in, L1_attn_b_in, L1_attn_W_out, L1_attn_b_out, L1_ffn_w1, L1_ffn_w2, L1_ffn_w3):

    def _L0_attn_ref(x, W_Q, W_K, W_V, W_O):
        import jax, jax.numpy as jnp
        import numpy as np
        EMB = 256
        HEADS = 16
        G = 2
        HEAD_DIM = EMB // HEADS
        KV = HEADS // G
        B = 2
        S = 256

        def compute_rope(x):
            D = x.shape[2]
            half = D // 2
            inv_freq = 1.0 / 10000.0 ** (jnp.arange(0, half, dtype=jnp.float32) * 2.0 / D)
            pos = jnp.arange(x.shape[1], dtype=jnp.float32)
            ang = pos[:, None] * inv_freq[None, :]
            cos = jnp.concatenate([jnp.cos(ang), jnp.cos(ang)], axis=-1)[None, :, :, None]
            sin = jnp.concatenate([jnp.sin(ang), jnp.sin(ang)], axis=-1)[None, :, :, None]
            x1, x2 = (x[:, :, :half], x[:, :, half:])
            rot = jnp.concatenate([-x2, x1], axis=2)
            return x * cos + rot * sin
        Bsz, Sl, E = x.shape
        q = (x @ W_Q.T).reshape(Bsz, Sl, HEAD_DIM, HEADS)
        k = (x @ W_K.T).reshape(Bsz, Sl, HEAD_DIM, KV)
        v = (x @ W_V.T).reshape(Bsz, Sl, HEAD_DIM, KV)
        q = compute_rope(q)
        k = compute_rope(k)
        q = q.reshape(Bsz, Sl, HEAD_DIM, KV, G)
        scores = jnp.einsum('bsdkg,btdk->bkgst', q, k) / jnp.sqrt(jnp.float32(E))
        w = jax.nn.softmax(scores, axis=-1)
        ctx = jnp.einsum('bkgst,btdk->bkgsd', w, v)
        ctx = ctx.reshape(Bsz, HEADS, Sl, HEAD_DIM).transpose(0, 2, 1, 3).reshape(Bsz, Sl, E)
        return ctx @ W_O.T

    def _L0_ffn_ref(x, gate_w, router_bias, W1, W3, W2, sw1, sw3, sw2):
        import jax, jax.numpy as jnp
        import numpy as np
        E = 8
        K = 2
        DIM = 256
        INTER = 176
        N_SHARED = 2
        STD = 0.02
        B, S, D = x.shape
        X = x.reshape(-1, D)
        T = X.shape[0]
        logits = jnp.einsum('td,ed->te', X, gate_w)
        scores = jax.nn.sigmoid(logits)
        sel = scores + router_bias[None, :]
        _, idx = jax.lax.top_k(sel, K)
        w = jnp.take_along_axis(scores, idx, axis=1)
        w = w / jnp.clip(jnp.sum(w, axis=-1, keepdims=True), 1e-12)
        gate_full = jnp.zeros((T, E), dtype=w.dtype).at[jnp.arange(T)[:, None], idx].set(w)
        h1 = jnp.einsum('td,edh->eth', X, W1)
        h3 = jnp.einsum('td,edh->eth', X, W3)
        y = jnp.einsum('eth,ehd->etd', jax.nn.silu(h1) * h3, W2)
        out = jnp.einsum('etd,te->td', y, gate_full)
        shared = jnp.einsum('th,dh->td', jax.nn.silu(jnp.einsum('td,hd->th', X, sw1)) * jnp.einsum('td,hd->th', X, sw3), sw2)
        out = out + shared
        return out.reshape(B, S, D)

    def _L1_attn_ref(X, W_in, b_in, W_out, b_out):
        import jax, jax.numpy as jnp
        import numpy as np
        ROPE_THETA = 10000.0

        def rope(t, rot_dim):
            S = t.shape[-2]
            half = rot_dim // 2
            inv_freq = 1.0 / ROPE_THETA ** (jnp.arange(0, rot_dim, 2, dtype=jnp.float32) / rot_dim)
            freqs = jnp.arange(S, dtype=jnp.float32)[:, None] * inv_freq[None, :]
            freqs = jnp.repeat(freqs, 2, axis=-1)
            cos, sin = (jnp.cos(freqs), jnp.sin(freqs))
            t_rot, t_pass = (t[..., :rot_dim], t[..., rot_dim:])
            x = t_rot.reshape(*t_rot.shape[:-1], half, 2)
            rh = jnp.stack([-x[..., 1], x[..., 0]], axis=-1).reshape(t_rot.shape)
            t_rot = t_rot * cos + rh * sin
            return jnp.concatenate([t_rot, t_pass], axis=-1)

        def feature_map(x):
            norm = jnp.sqrt(jnp.sum(x * x, axis=-1, keepdims=True))
            return x / jnp.maximum(norm, 1e-12)
        D = X.shape[-1]
        QKV = jnp.einsum('bsd,ed->bse', X, W_in) + b_in
        Q, K, V = jnp.split(QKV, 3, axis=-1)
        rot_dim = D // 2
        Q = rope(Q, rot_dim)
        K = rope(K, rot_dim)
        A = jnp.sum(feature_map(K) * V, axis=-2)
        Y = A[:, None, :] * Q
        Y = jnp.einsum('bsd,ed->bse', Y, W_out) + b_out
        return Y + X

    def _L1_ffn_ref(x, w1, w2, w3):
        import jax, jax.numpy as jnp
        import numpy as np
        EPS = 1e-08

        def _quantize(w):
            gamma = jnp.mean(jnp.abs(w))
            return jnp.clip(jnp.round(w / (gamma + EPS)), -1.0, 1.0)

        def _bitlinear(x, w):
            return jnp.matmul(x, _quantize(w).T)
        x1 = _bitlinear(x, w1)
        x2 = _bitlinear(x, w2)
        hidden = jax.nn.sigmoid(x1) * x2
        return _bitlinear(hidden, w3)
    x = L0_attn_x
    x = x + _L0_attn_ref(_layernorm(x, axis=-1), L0_attn_W_Q, L0_attn_W_K, L0_attn_W_V, L0_attn_W_O)
    x = x + _L0_ffn_ref(_layernorm(x, axis=-1), L0_ffn_gate_w, L0_ffn_router_bias, L0_ffn_W1, L0_ffn_W3, L0_ffn_W2, L0_ffn_sw1, L0_ffn_sw3, L0_ffn_sw2)
    x = x + _L1_attn_ref(_layernorm(x, axis=-1), L1_attn_W_in, L1_attn_b_in, L1_attn_W_out, L1_attn_b_out)
    x = x + _L1_ffn_ref(_layernorm(x, axis=-1), L1_ffn_w1, L1_ffn_w2, L1_ffn_w3)
    return x

_drawn_inputs = setup_inputs


def setup_inputs(seed=0):
    import zlib

    import numpy as np

    out = dict(_drawn_inputs(seed))
    spreads = {'L0_ffn_router_bias': (0.0, 0.585),
     'L1_attn_b_in': (0.0, 0.1),
     'L1_attn_b_out': (0.0, 0.1)}
    factors = {'L0_attn_W_Q': 8.0,
     'L0_attn_W_K': 8.0,
     'L0_attn_W_V': 5.375,
     'L0_attn_W_O': 5.39,
     'L0_ffn_gate_w': 4.187,
     'L0_ffn_W1': 3.399,
     'L0_ffn_W3': 3.362,
     'L0_ffn_W2': 3.356}
    for name, (base, spread) in spreads.items():
        noise = np.random.default_rng([zlib.crc32(name.encode()), seed]).standard_normal(out[name].shape)
        drawn = base * np.exp(spread * noise) if base else spread * noise
        out[name] = jnp.asarray(drawn.astype(out[name].dtype))
    for name, factor in factors.items():
        out[name] = (out[name] * factor).astype(out[name].dtype)
    return out
```

```python
from contextlib import ExitStack

import numpy as np

import concourse.bass as bass
from concourse import mybir

F32 = mybir.dt.float32
F32R = mybir.dt.float32r
U32 = mybir.dt.uint32
ALU = mybir.AluOpType
ACT = mybir.ActivationFunctionType
AX = mybir.AxisListType

P = 128
D = 256
KD = D // P
BATCHES = 8
S = 256
NT = S // P
HEADS, KV, G, DH = 16, 8, 2, 16
EXPERTS, INTER, SHARED = 8, 176, 2
GROUPS = SHARED + EXPERTS
HID = GROUPS * INTER
CHUNKS = -(-HID // P)
FFN_HID = 704
FGROUPS = FFN_HID // INTER
FCHUNKS = -(-FFN_HID // P)
PAIR = 2 * INTER
W13 = GROUPS * PAIR + EXPERTS
LN_EPS = 1e-5
NORM_EPS2 = 1e-24
QUANT_EPS = 1e-8

O_QKV = 0
O_WO = O_QKV + KD * (D + 2 * P)
O_W13 = O_WO + KD * D
O_W2 = O_W13 + KD * W13
O_WIN = O_W2 + CHUNKS * D
O_WOUT = O_WIN + KD * 3 * D
WCOLS = O_WOUT + KD * D
PIECES = 8
PW = -(-(WCOLS - O_W13) // PIECES)
WCUTS = [0, O_W13] + [min(O_W13 + PW * (n + 1), WCOLS) for n in range(PIECES)]
TW = KD * FFN_HID
STAGE = max(PW, FCHUNKS * D, TW, O_W13)
SLOTS = 3

ZSTEP = P
ZHALF = 3 * P + 2 * DH
ZCOLS = 2 * ZHALF + DH


def zwindow(head):
    kv = head // G
    return (kv // 4) * ZHALF + DH + ZSTEP * (kv % 4) - DH * (head % 8)


def group_start(gi):
    return gi * PAIR + (EXPERTS if gi else 0)


def build(nc, x, wpack, tern1, tern2, tern3, rbias, b_in, b_out, rope0, rope1, eye, out):
    ctx = ExitStack()
    with ctx:
        def sb(name, cols, dt=F32, where=ctx):
            return where.enter_context(nc.sbuf_tensor(name, [P, cols], dt))

        def sem(name):
            return ctx.enter_context(nc.semaphore(name))

        w_hi = sb("w_hi", WCOLS, F32R)
        w_lo = sb("w_lo", WCOLS, F32R)
        w12q = sb("w12q", 2 * TW, F32R)
        w3q = sb("w3q", FCHUNKS * D, F32R)
        ident = sb("ident", P)
        ones = sb("ones", P)
        cos0 = sb("rope0_sb", 2 * NT * 192)
        cs1 = sb("rope1_sb", 2 * NT * 64)
        bin_sb = sb("bin_sb", 3 * D)
        bout_sb = sb("bout_sb", D)
        rb_sb = sb("rb_sb", EXPERTS)
        mhalf = sb("mhalf", NT)
        epst = sb("epst", NT)
        iot = sb("iot", EXPERTS)
        fence = sb("fence", 2)
        a_st = sb("a_st", NT * 6)
        a_mv = sb("a_mv", NT * 2)
        a_ve = sb("a_ve", NT)
        a_rstd = sb("a_rstd", NT)
        nmax = [sb(f"nmax{i}", NT) for i in range(2)]
        rsum = [sb(f"rsum{i}", NT) for i in range(2)]
        rrec = [sb(f"rrec{i}", NT) for i in range(2)]
        b_st = sb("b_st", NT * 6)
        b_mv = sb("b_mv", NT * 2)
        b_ve = sb("b_ve", NT)
        b_rstd = sb("b_rstd", NT)
        r_e = sb("r_e", EXPERTS)
        r_sc = sb("r_sc", EXPERTS)
        r_sel = sb("r_sel", EXPERTS)
        r_top = sb("r_top", 8)
        r_idx = sb("r_idx", 8, U32)
        r_idf = sb("r_idf", 8)
        r_m = sb("r_m", EXPERTS)
        r_sum = sb("r_sum", 4)
        gate = sb("gate", EXPERTS)
        ssq = sb("ssq", NT)
        ssm = sb("ssm", NT)
        krn = sb("krn", NT)
        asum = sb("asum", 3)
        thr = sb("thr", 3 * 2)

        xA = sb("xA", NT * D)
        qT = sb("qT", 8 * S, F32R)
        kT = sb("kT", 4 * S, F32R)
        z_hi = sb("z_hi", NT * ZCOLS, F32R)
        z_lo = sb("z_lo", NT * ZCOLS, F32R)
        with ExitStack() as early:
            ahT_hi = sb("ahT_hi", NT * D, F32R, early)
            ahT_lo = sb("ahT_lo", NT * D, F32R, early)
            hA = sb("hA", NT * D, F32, early)
            t1A = sb("t1A", 384, F32, early)
            t2A = sb("t2A", 384, F32, early)
            qs = sb("qs", 1024, F32R, early)
            ks = sb("ks", 512, F32R, early)
        cT_hi = sb("cT_hi", NT * D, F32R)
        cT_lo = sb("cT_lo", NT * D, F32R)
        pr = [sb(f"pr{i}", NT * S) for i in range(2)]
        pT_hi = [sb(f"pT_hi{i}", NT * S, F32R) for i in range(2)]
        pT_lo = [sb(f"pT_lo{i}", NT * S, F32R) for i in range(2)]

        with ExitStack() as prep:
            stage = [sb(f"stage{i}", STAGE, F32, prep) for i in range(SLOTS)]
        xB = sb("xB", NT * D)
        hB = sb("hB", NT * D)
        bhT_hi = sb("bhT_hi", NT * D, F32R)
        bhT_lo = sb("bhT_lo", NT * D, F32R)
        hid = sb("hid", HID)
        th = [sb(f"th{i}", 256) for i in range(2)]
        hdT_hi = [sb(f"hdT_hi{i}", 512, F32R) for i in range(2)]
        hdT_lo = [sb(f"hdT_lo{i}", 512, F32R) for i in range(2)]

        bank = [ctx.enter_context(nc.psum_tensor(f"bank{i}", [P, 512], F32)) for i in range(8)]
        bS, bPT, bC = bank[0:2], bank[2], bank[3]
        bG, bTB, bY = bank[4:6], bank[6], bank[7]

        def v2(t, a):
            return t[:, :].rearrange("p (a n) -> p a n", a=a)

        x_t, xA_t, xB_t, hA_t, hB_t = (v2(t, NT) for t in (xA, xA, xB, hA, hB))
        cosr = cos0[:, :].rearrange("p (f t h j) -> p f t h j", f=2, t=NT, j=8)
        c1r = cs1[:, :].rearrange("p (f t j) -> p f t j", f=2, t=NT)
        x_b = x.rearrange("b (t p) d -> b p t d", p=P)
        out_b = out.rearrange("b (t p) d -> b p t d", p=P)

        def W(part, at, k, width, a, b):
            return part[:, at + k * width + a:at + k * width + b]

        stage_in = [sem(f"stage_in{i}") for i in range(SLOTS)]
        consts_in, x_in, xB_free = sem("consts_in"), sem("x_in"), sem("xB_free")
        setup_pool, zeros_ready = sem("setup_pool"), sem("zeros_ready")
        split_hi, split_lo = sem("split_hi"), sem("split_lo")
        abs_sum, abs_total, tern_done, quant_chain = sem("abs_sum"), sem("abs_total"), sem("tern_done"), sem("quant_chain")
        a_chain, a_mv_r, a_ve_r, a_rstd_r, a_h_r = (sem(f"a_{n}") for n in ("chain", "mv_r", "ve_r", "rstd_r", "h_r"))
        a_hps, a_hhi, a_hlo = sem("a_hps"), sem("a_hhi"), sem("a_hlo")
        a_qkv, a_rope, a_zhi, a_zlo, a_sthi, a_stlo = (sem(f"a_{n}") for n in ("qkv", "rope", "zhi", "zlo", "sthi", "stlo"))
        a_stT, a_stev_act, a_stev_dve = sem("a_stT"), sem("a_stev_act"), sem("a_stev_dve")
        a_score, a_nmax, a_exp, a_rrec, a_prob = (sem(f"a_{n}") for n in ("score", "nmax", "exp", "rrec", "prob"))
        a_pps, a_phi, a_plo, a_pv = (sem(f"a_{n}") for n in ("pps", "phi", "plo", "pv"))
        a_chi, a_clo, a_wo, a_xmid = (sem(f"a_{n}") for n in ("chi", "clo", "wo", "xmid"))
        b_chain, b_xcopy, b_mv_r, b_ve_r, b_rstd_r, b_h_r = (sem(f"b_{n}") for n in ("chain", "xcopy", "mv_r", "ve_r", "rstd_r", "h_r"))
        b_hps, b_hhi, b_hlo = sem("b_hps"), sem("b_hhi"), sem("b_hlo")
        b_grp, b_route, b_gate, b_th, b_hid = (sem(f"b_{n}") for n in ("grp", "route", "gate", "th", "hid"))
        b_tps, b_thi, b_tlo, b_down, b_res1 = (sem(f"b_{n}") for n in ("tps", "thi", "tlo", "down", "res1"))
        b_qkv, b_qkvev, b_ssq, b_ssm, b_krn, b_kv, b_A, b_y = (sem(f"b_{n}") for n in ("qkv", "qkvev", "ssq", "ssm", "krn", "kv", "A", "y"))
        b_attn, b_hb, b_res, b_fin = (sem(f"b_{n}") for n in ("attn", "hb", "res", "fin"))

        def at(b, per, k):
            return b * per + k

        NLN = 3
        NG = NT * (GROUPS + FGROUPS)
        TQ, FQ = -(-CHUNKS // 4), -(-FCHUNKS // 4)
        NQ = NT * (TQ + FQ)

        def chunks_of(n_hid, q):
            return [(c, min(P, n_hid - c * P)) for c in range(4 * q, min(4 * q + 4, -(-n_hid // P)))]

        ctx2 = ctx.enter_context(nc.Block())
        block = ctx2

        def vview(ps, u):
            a = D + P + u * 4 * DH
            return ps[:, a:a + 4 * DH].rearrange("p (v d) -> p v d", d=DH)

        def zview(z, t, u):
            first, step = 1 + u * (ZHALF // DH), ZSTEP // DH
            return z[:, t * ZCOLS:(t + 1) * ZCOLS].rearrange("p (c d) -> p c d", d=DH)[:, first:first + 3 * step + 1:step, :]

        def stack_dst(j, t):
            dst = qT if j < 2 else kT
            a = 4 * j if j < 2 else 0
            return dst[:, :].rearrange("p (k n) -> p k n", n=S)[:, a:a + 4, t * P:(t + 1) * P]

        def down_after(n, q, n_hid):
            need = min(-(-(4 * q + 4) * P // INTER), n) - 1
            return min(need + 1, n - 1)

        def run(eng, stream_a, stream_b):
            with eng.Fori(0, BATCHES) as b:
                for _ in stream_a(b):
                    pass
                for _ in stream_b(b):
                    pass

        @block.sync
        def _(sp):
            sp.dma_start(stage[0][:, 0:WCUTS[1]], wpack[:, 0:WCUTS[1]]).then_inc(stage_in[0], 16)
            sp.dma_start(xA_t, x_b[0]).then_inc(x_in, 16)
            for t, src in ((ident, eye), (cos0, rope0), (cs1, rope1)):
                sp.dma_start(t[:, :], src).then_inc(consts_in, 16)
            for t, src, n in ((bin_sb, b_in, 3 * D), (bout_sb, b_out, D), (rb_sb, rbias, EXPERTS)):
                sp.dma_start(t[:, :], src.rearrange("(a n) -> a n", a=1).broadcast_to([P, n])).then_inc(consts_in, 16)
            for n in range(1, PIECES + 1):
                if n >= SLOTS:
                    sp.wait_ge(split_lo, n - SLOTS + 1)
                a, b = WCUTS[n], WCUTS[n + 1]
                sp.dma_start(stage[n % SLOTS][:, 0:b - a], wpack[:, a:b]).then_inc(stage_in[n % SLOTS], 16)
            for j, (src, w) in enumerate(((tern1, TW), (tern2, TW), (tern3, FCHUNKS * D))):
                n = PIECES + 1 + j
                sp.wait_ge(split_lo, n - SLOTS + 1)
                sp.dma_start(stage[n % SLOTS][:, 0:w], src).then_inc(stage_in[n % SLOTS], 16)
            def load_x(b):
                sp.wait_ge(b_xcopy, at(b - 1, 1, 1))
                sp.dma_start(xA_t, x_b[b]).then_inc(x_in, 16)

            def store(b):
                sp.wait_ge(b_fin, at(b, NT, NT))
                sp.dma_start(out_b[b], xB_t).then_inc(xB_free, 16)

            with sp.Fori(1, BATCHES) as b:
                load_x(b)
                store(b - 1)
            store(BATCHES - 1)
            sp.wait_ge(xB_free, 16 * (BATCHES + 1))

        @block.gpsimd
        def _(pool):
            nc.gpsimd.memset(ones[:, :], 1.0).then_inc(setup_pool, 1)
            nc.gpsimd.memset(fence[:, 1:2], 0.0).then_inc(xB_free, 16)
            nc.gpsimd.memset(mhalf[:, :], -0.5).then_inc(setup_pool, 1)
            nc.gpsimd.memset(epst[:, :], LN_EPS).then_inc(setup_pool, 1)
            nc.gpsimd.iota(iot[:, :], pattern=[[1, EXPERTS]], base=0, channel_multiplier=0,
                           allow_small_or_imprecise_dtypes=True).then_inc(setup_pool, 1)
            pool.wait_ge(setup_pool, 4)

            def rstd(mv, ve, rs, s_mv, s_ve, s_rs, n_mv, n):
                pool.wait_ge(s_mv, n_mv)
                nc.gpsimd.tensor_tensor(ve[:, :], v2(mv, NT)[:, :, 1], epst[:, :], ALU.add).then_inc(s_ve, 1)
                pool.wait_ge(s_ve, n)
                nc.gpsimd.tensor_tensor(rs[:, :], ve[:, :], mhalf[:, :], ALU.pow).then_inc(s_rs, 1)

            def stream_a(b):
                rstd(a_mv, a_ve, a_rstd, a_mv_r, a_ve_r, a_rstd_r, at(b, NT, NT), at(b, 1, 1))
                yield
                for t in range(NT):
                    pool.wait_ge(a_sthi, at(b, NT, t + 1))
                    q4 = qs[:, :].rearrange("p (h s d) -> p h s d", s=4, d=DH)
                    k4 = ks[:, :].rearrange("p (h s d) -> p h s d", s=4, d=DH)
                    q1 = t1A[:, 0:D].rearrange("p (h o d) -> p h o d", o=1, d=DH)
                    k1 = t1A[:, D:D + P].rearrange("p (h o d) -> p h o d", o=1, d=DH)
                    nc.gpsimd.tensor_tensor(q4[:, :, 2:4, :], q1.broadcast_to([P, HEADS, 2, DH]),
                                            q4[:, :, 0:2, :], ALU.subtract)
                    nc.gpsimd.tensor_tensor(k4[:, :, 1:4:2, :], k1.broadcast_to([P, KV, 2, DH]),
                                            k4[:, :, 0:4:2, :], ALU.subtract).then_inc(a_stlo, 1)
                    yield
                for h in range(HEADS):
                    pool.wait_ge(a_rrec, at(b, HEADS, h + 1))
                    nc.gpsimd.tensor_tensor(v2(pr[h % 2], NT), v2(pr[h % 2], NT),
                                            rrec[h % 2][:, :].rearrange("p (t o) -> p t o", o=1).broadcast_to([P, NT, S]),
                                            ALU.mult).then_inc(a_prob, 1)
                    yield

            def norm_b(b, n):
                rstd(b_mv, b_ve, b_rstd, b_mv_r, b_ve_r, b_rstd_r, at(b, NLN * NT, NT * (n + 1)), at(b, NLN, n + 1))

            def stream_b(b):
                norm_b(b, 0)
                yield
                norm_b(b, 1)
                pool.wait_ge(b_ssm, at(b, 1, 1))
                nc.gpsimd.tensor_tensor(krn[:, :], ssm[:, :], mhalf[:, :], ALU.pow).then_inc(b_krn, 1)
                nc.gpsimd.tensor_tensor(hB_t, hB_t, bout_sb[:, :].rearrange("p (o n) -> p o n", o=1).broadcast_to([P, NT, D]),
                                        ALU.add).then_inc(b_hb, 1)
                pool.wait_ge(b_hb, at(b, 1, 1))
                nc.gpsimd.tensor_tensor(xB[:, :], xB[:, :], hB[:, :], ALU.add).then_inc(b_res, 1)
                yield
                norm_b(b, 2)
                yield

            run(pool, stream_a, stream_b)

        @block.scalar
        def _(act):
            act.wait_ge(consts_in, 16 * 6)
            for n in range(PIECES + 1):
                a, b = WCUTS[n], WCUTS[n + 1]
                act.wait_ge(stage_in[n % SLOTS], 16 * (n // SLOTS + 1))
                nc.scalar.activation(w_hi[:, a:b], stage[n % SLOTS][:, 0:b - a], ACT.Copy).then_inc(split_hi, 1)

            def split_h(b, ps, dst, s_ps, n_ps, s_hi):
                act.wait_ge(s_ps, n_ps)
                nc.scalar.activation(dst, ps, ACT.Copy).then_inc(s_hi, 1)

            def stream_a(b):
                split_h(b, bPT[:, :], ahT_hi[:, :], a_hps, at(b, 1, 1), a_hhi)
                yield
                for t in range(NT):
                    act.wait_ge(a_qkv, at(b, NT, t + 1))
                    for u in range(2):
                        ins = nc.scalar.activation(zview(z_hi, t, u), vview(bS[t], u), ACT.Copy)
                    ins.then_inc(a_zhi, 1)
                    act.wait_ge(a_rope, at(b, NT, t + 1))
                    q4 = qs[:, :].rearrange("p (h s d) -> p h s d", s=4, d=DH)
                    k4 = ks[:, :].rearrange("p (h s d) -> p h s d", s=4, d=DH)
                    q1 = t1A[:, 0:D].rearrange("p (h o d) -> p h o d", o=1, d=DH)
                    k1 = t1A[:, D:D + P].rearrange("p (h o d) -> p h o d", o=1, d=DH)
                    if t > 0:
                        act.wait_ge(a_stT, at(b, 3 * NT, 3 * t))
                    nc.scalar.activation(q4[:, :, 0:2, :], q1.broadcast_to([P, HEADS, 2, DH]), ACT.Copy)
                    nc.scalar.activation(k4[:, :, 0:4:2, :], k1.broadcast_to([P, KV, 2, DH]), ACT.Copy).then_inc(a_sthi, 1)
                    for j in range(3):
                        n = 3 * t + j
                        if n % 2 == 0:
                            act.wait_ge(a_stT, at(b, 3 * NT, n + 1))
                            nc.scalar.activation(stack_dst(j, t), v2(bPT, 4), ACT.Copy).then_inc(a_stev_act, 1)
                    yield
                for h in range(HEADS + 1):
                    if h < HEADS:
                        act.wait_ge(a_nmax, at(b, HEADS, h + 1))
                        if h >= 2:
                            act.wait_ge(a_pps, at(b, HEADS, h - 1))
                        for st in range(NT):
                            ins = nc.scalar.activation(pr[h % 2][:, st * S:(st + 1) * S], bS[h % 2][:, st * S:(st + 1) * S], ACT.Exp,
                                                       bias=nmax[h % 2][:, st:st + 1], accum_out=rsum[h % 2][:, st:st + 1])
                        ins.then_inc(a_exp, 1)
                    if h >= 1:
                        if h >= 3:
                            act.wait_ge(a_pv, at(b, HEADS, h - 2))
                        split_h(b, bPT[:, :], pT_hi[(h - 1) % 2][:, :], a_pps, at(b, HEADS, h), a_phi)
                    yield
                split_h(b, bC[:, :], cT_hi[:, :], a_pv, at(b, HEADS, HEADS), a_chi)
                yield

            def groups(b, t, n, first, routed):
                for gi in range(n):
                    m = first + t * n + gi
                    act.wait_ge(b_grp, at(b, NG, m + 1))
                    if routed and gi == 0:
                        nc.scalar.activation(r_e[:, :], bG[m % 2][:, PAIR:PAIR + EXPERTS], ACT.Exp, scale=-1.0).then_inc(b_route, 1)
                    nc.scalar.activation(th[m % 2][:, 0:INTER], bG[m % 2][:, 0:INTER], ACT.Tanh, scale=0.5).then_inc(b_th, 1)
                    yield gi

            def down(b, m, cols):
                if m >= 2:
                    act.wait_ge(b_down, at(b, NQ, m - 1))
                split_h(b, bTB[:, 0:cols], hdT_hi[m % 2][:, 0:cols], b_tps, at(b, NQ, m + 1), b_thi)

            def stream_b(b):
                act.wait_ge(a_xmid, at(b, 1, 1))
                act.wait_ge(xB_free, at(b, 16, 16))
                nc.scalar.activation(xB[:, :], xA[:, :], ACT.Copy).then_inc(b_xcopy, 1)
                split_h(b, bTB[:, :], bhT_hi[:, :], b_hps, at(b, NLN + 1, 1), b_hhi)
                yield
                for t in range(NT):
                    for gi in groups(b, t, GROUPS, 0, True):
                        for q in range(TQ):
                            if down_after(GROUPS, q, HID) == gi:
                                down(b, t * TQ + q, P * len(chunks_of(HID, q)))
                        yield
                split_h(b, bTB[:, :], bhT_hi[:, :], b_hps, at(b, NLN + 1, 2), b_hhi)
                yield
                split_h(b, bTB[:, :], bhT_hi[:, :], b_hps, at(b, NLN + 1, 3), b_hhi)
                yield
                split_h(b, bTB[:, :], bhT_hi[:, :], b_hps, at(b, NLN + 1, 4), b_hhi)
                yield
                for t in range(NT):
                    for gi in groups(b, t, FGROUPS, NT * GROUPS, False):
                        for q in range(FQ):
                            if down_after(FGROUPS, q, FFN_HID) == gi:
                                down(b, NT * TQ + t * FQ + q, P * len(chunks_of(FFN_HID, q)))
                        yield

            run(act, stream_a, stream_b)

        @block.vector
        def _(dve):
            A_LINKS = 1 + NT
            B_LINKS = NLN + NT * (GROUPS + 12) + NT * 2 + 1
            links = {"a": 0, "b": 0}
            chain = {"a": a_chain, "b": b_chain}

            def link(s, b, per, ins):
                links[s] += 1
                ins.then_inc(chain[s], 1)
                dve.wait_ge(chain[s], at(b, per, links[s]))

            for n in range(PIECES + 1):
                a, b = WCUTS[n], WCUTS[n + 1]
                dve.wait_ge(split_hi, n + 1)
                nc.vector.tensor_tensor(w_lo[:, a:b], stage[n % SLOTS][:, 0:b - a], w_hi[:, a:b], ALU.subtract).then_inc(split_lo, 1)
                if n == 0:
                    nc.vector.memset(z_hi[:, :].bitcast(F32), 0.0).then_inc(zeros_ready, 1)
                    nc.vector.memset(z_lo[:, :].bitcast(F32), 0.0).then_inc(zeros_ready, 1)
                    dve.wait_ge(zeros_ready, 2)
            for j, w in enumerate((TW, TW, FCHUNKS * D)):
                n = PIECES + 1 + j
                dve.wait_ge(stage_in[n % SLOTS], 16 * (n // SLOTS + 1))
                nc.vector.tensor_reduce(asum[:, j:j + 1], stage[n % SLOTS][:, 0:w], AX.X, ALU.add,
                                        apply_absolute_value=True).then_inc(abs_sum, 1)
            dve.wait_ge(abs_total, 1)
            nc.vector.tensor_scalar(thr[:, 0:3], bY[:, 0:3], 1.0 / (FFN_HID * D), QUANT_EPS, ALU.mult, ALU.add).then_inc(quant_chain, 1)
            dve.wait_ge(quant_chain, 1)
            nc.vector.tensor_scalar(thr[:, 3:6], thr[:, 0:3], -0.5, None, ALU.mult).then_inc(quant_chain, 1)
            dve.wait_ge(quant_chain, 2)
            nc.vector.tensor_scalar(thr[:, 0:3], thr[:, 0:3], 0.5, None, ALU.mult).then_inc(quant_chain, 1)
            dve.wait_ge(quant_chain, 3)
            nq = 3
            for j in range(3):
                src = stage[(PIECES + 1 + j) % SLOTS]
                for k in range(KD if j < 2 else 1):
                    w = FFN_HID if j < 2 else FCHUNKS * D
                    s = src[:, k * w:(k + 1) * w]
                    if j < 2:
                        s = s.rearrange("p (g n) -> p g n", n=INTER)
                        d = w12q[:, :].rearrange("p (k g u n) -> p k g u n", k=KD, g=FGROUPS, u=2)[:, k, :, j, :]
                    else:
                        d = w3q[:, :]
                    nc.vector.tensor_scalar(d, s, thr[:, 3 + j:4 + j], None, ALU.is_lt).then_inc(quant_chain, 1)
                    nq += 1
                    dve.wait_ge(quant_chain, nq)
                    nc.vector.scalar_tensor_tensor(out=d, in0=s, scalar=thr[:, j:j + 1], in1=d.bitcast(F32), op0=ALU.is_gt,
                                                   op1=ALU.subtract).then_inc(tern_done, 1)
            dve.wait_ge(tern_done, 2 * KD + 1)

            def hold():
                nc.vector.memset(fence[:, 0:1], 0.0)

            def stats(s, b, per, xt, st, mv, s_mv):
                for t in range(NT):
                    ins = nc.vector.bn_stats(st[:, 6 * t:6 * t + 6], xt[:, t, :])
                link(s, b, per, ins)
                hold()
                for t in range(NT):
                    nc.vector.bn_aggr(mv[:, 2 * t:2 * t + 2], st[:, 6 * t:6 * t + 6]).then_inc(s_mv, 1)

            def normalise(xt, ht, mv, rs, s_rs, n, s_h):
                dve.wait_ge(s_rs, n)
                for t in range(NT):
                    nc.vector.tensor_scalar(ht[:, t, :], xt[:, t, :], mv[:, 2 * t:2 * t + 1], rs[:, t:t + 1],
                                            ALU.subtract, ALU.mult).then_inc(s_h, 1)

            def split_l(ps, hi, dst, s_hi, n_hi, s_lo):
                dve.wait_ge(s_hi, n_hi)
                nc.vector.tensor_tensor(dst, ps, hi.bitcast(F32), ALU.subtract).then_inc(s_lo, 1)

            def stream_a(b):
                links["a"] = 0
                dve.wait_ge(x_in, at(b, 16, 16))
                stats("a", b, A_LINKS, xA_t, a_st, a_mv, a_mv_r)
                normalise(xA_t, hA_t, a_mv, a_rstd, a_rstd_r, at(b, 1, 1), a_h_r)
                yield
                split_l(bPT[:, :], ahT_hi[:, :], ahT_lo[:, :], a_hhi, at(b, 1, 1), a_hlo)
                yield
                for t in range(NT):
                    dve.wait_ge(a_zhi, at(b, NT, t + 1))
                    src = bS[t][:, 0:384].rearrange("p (h e j) -> p h e j", e=2, j=8)
                    t1 = t1A[:, :].rearrange("p (h e j) -> p h e j", e=2, j=8)
                    t2 = t2A[:, :].rearrange("p (h e j) -> p h e j", e=2, j=8)
                    cosb = cosr[:, 0, t].rearrange("p h (o j) -> p h o j", o=1).broadcast_to([P, 24, 2, 8])
                    if t > 0:
                        dve.wait_ge(a_stlo, at(b, NT, t))
                    nc.vector.tensor_tensor(t1, src, cosb, ALU.mult)
                    nc.vector.scalar_tensor_tensor(out=t2[:, :, 0, :], in0=src[:, :, 1, :], scalar=-1.0, in1=cosr[:, 1, t],
                                                   op0=ALU.mult, op1=ALU.mult)
                    link("a", b, A_LINKS, nc.vector.tensor_tensor(t2[:, :, 1, :], src[:, :, 0, :], cosr[:, 1, t], ALU.mult))
                    nc.vector.tensor_tensor(t1A[:, :], t1A[:, :], t2A[:, :], ALU.add).then_inc(a_rope, 1)
                    for u in range(2):
                        ins = nc.vector.tensor_tensor(zview(z_lo, t, u), vview(bS[t], u), zview(z_hi, t, u).bitcast(F32), ALU.subtract)
                    ins.then_inc(a_zlo, 1)
                    for j in range(3):
                        n = 3 * t + j
                        if n % 2 == 1:
                            dve.wait_ge(a_stT, at(b, 3 * NT, n + 1))
                            nc.vector.tensor_copy(stack_dst(j, t), v2(bC, 4)).then_inc(a_stev_dve, 1)
                    yield
                for h in range(HEADS + 2):
                    if h < HEADS:
                        dve.wait_ge(a_score, at(b, HEADS, h + 1))
                        nc.vector.tensor_reduce(nmax[h % 2][:, :], v2(bS[h % 2], NT), AX.X, ALU.max, negate=True).then_inc(a_nmax, 1)
                    if 1 <= h <= HEADS:
                        dve.wait_ge(a_exp, at(b, HEADS, h))
                        nc.vector.reciprocal(rrec[(h - 1) % 2][:, :], rsum[(h - 1) % 2][:, :]).then_inc(a_rrec, 1)
                    if h >= 2:
                        split_l(bPT[:, :], pT_hi[h % 2][:, :], pT_lo[h % 2][:, :], a_phi, at(b, HEADS, h - 1), a_plo)
                    yield
                split_l(bC[:, :], cT_hi[:, :], cT_lo[:, :], a_chi, at(b, 1, 1), a_clo)
                yield
                dve.wait_ge(a_wo, at(b, 1, 1))
                nc.vector.tensor_tensor(xA[:, :], bS[0][:, :], xA[:, :], ALU.add).then_inc(a_xmid, 1)
                yield

            def lnk(b, ins):
                link("b", b, B_LINKS, ins)

            def route(b, t):
                dve.wait_ge(b_route, at(b, NT, t + 1))
                lnk(b, nc.vector.tensor_scalar(r_sc[:, :], r_e[:, :], 1.0, None, ALU.add))
                lnk(b, nc.vector.reciprocal(r_sc[:, :], r_sc[:, :]))
                lnk(b, nc.vector.tensor_tensor(r_sel[:, :], r_sc[:, :], rb_sb[:, :], ALU.add))
                hold()
                lnk(b, nc.vector.max(r_top[:, :], r_sel[:, :]))
                hold()
                lnk(b, nc.vector.max_index(r_idx[:, :], r_top[:, :], r_sel[:, :]))
                lnk(b, nc.vector.tensor_copy(r_idf[:, :], r_idx[:, :]))
                lnk(b, nc.vector.tensor_scalar(r_m[:, :], iot[:, :], r_idf[:, 0:1], None, ALU.is_equal))
                lnk(b, nc.vector.scalar_tensor_tensor(out=r_m[:, :], in0=iot[:, :], scalar=r_idf[:, 1:2], in1=r_m[:, :],
                                                      op0=ALU.is_equal, op1=ALU.add))
                lnk(b, nc.vector.tensor_tensor_reduce(r_m[:, :], r_m[:, :], r_sc[:, :], 1.0, 0.0, ALU.mult, ALU.add, r_sum[:, 0:1]))
                lnk(b, nc.vector.tensor_scalar(r_sum[:, 1:2], r_sum[:, 0:1], 1e-12, None, ALU.max))
                lnk(b, nc.vector.reciprocal(r_sum[:, 2:3], r_sum[:, 1:2]))
                lnk(b, nc.vector.tensor_scalar(gate[:, :], r_m[:, :], r_sum[:, 2:3], 0.5, ALU.mult, ALU.mult))

            def groups(b, t, n, first, routed):
                for gi in range(n):
                    m = first + t * n + gi
                    g = bG[m % 2]
                    u, v = th[m % 2][:, 0:INTER], hid[:, gi * INTER:(gi + 1) * INTER]
                    dve.wait_ge(b_th, at(b, NG, m + 1))
                    if routed:
                        lnk(b, nc.vector.scalar_tensor_tensor(out=u, in0=u, scalar=1.0, in1=g[:, 0:INTER], op0=ALU.add, op1=ALU.mult))
                        half = 0.5 if gi < SHARED else gate[:, gi - SHARED:gi - SHARED + 1]
                        nc.vector.scalar_tensor_tensor(out=v, in0=u, scalar=half, in1=g[:, INTER:PAIR], op0=ALU.mult,
                                                       op1=ALU.mult).then_inc(b_hid, 1)
                        if gi == 0:
                            route(b, t)
                    else:
                        nc.vector.scalar_tensor_tensor(out=v, in0=u, scalar=1.0, in1=g[:, INTER:PAIR], op0=ALU.add,
                                                       op1=ALU.mult).then_inc(b_hid, 1)
                    yield gi

            def down(b, m, cols):
                split_l(bTB[:, 0:cols], hdT_hi[m % 2][:, 0:cols], hdT_lo[m % 2][:, 0:cols], b_thi, at(b, NQ, m + 1), b_tlo)

            def norm_b(b, n):
                stats("b", b, B_LINKS, xB_t, b_st, b_mv, b_mv_r)
                normalise(xB_t, hB_t, b_mv, b_rstd, b_rstd_r, at(b, NLN, n + 1), b_h_r)

            def stream_b(b):
                links["b"] = 0
                dve.wait_ge(b_xcopy, at(b, 1, 1))
                norm_b(b, 0)
                yield
                split_l(bTB[:, :], bhT_hi[:, :], bhT_lo[:, :], b_hhi, at(b, NLN + 1, 1), b_hlo)
                yield
                for t in range(NT):
                    for gi in groups(b, t, GROUPS, 0, True):
                        for q in range(TQ):
                            if down_after(GROUPS, q, HID) == gi:
                                down(b, t * TQ + q, P * len(chunks_of(HID, q)))
                        yield
                    dve.wait_ge(b_down, at(b, NQ, (t + 1) * TQ))
                    nc.vector.tensor_tensor(xB_t[:, t, :], bY[:, 0:D], xB_t[:, t, :], ALU.add).then_inc(b_res1, 1)
                    yield
                dve.wait_ge(b_res1, at(b, NT, NT))
                norm_b(b, 1)
                yield
                split_l(bTB[:, :], bhT_hi[:, :], bhT_lo[:, :], b_hhi, at(b, NLN + 1, 2), b_hlo)
                yield
                qk_all = hid[:, 0:NT * 2 * D].rearrange("p (t u n) -> p t u n", t=NT, u=2)
                kv = hid[:, NT * 2 * D:NT * 3 * D].rearrange("p (t n) -> p t n", t=NT)
                for t in range(NT):
                    qk = qk_all[:, t]
                    dve.wait_ge(b_qkv, at(b, NT, t + 1))
                    nc.vector.tensor_tensor(kv[:, t], bG[1][:, 0:D], bin_sb[:, 2 * D:3 * D], ALU.add)
                    link_ = nc.vector.tensor_tensor(qk, v2(bG[0], 2), bin_sb[:, 0:2 * D].rearrange("p (u n) -> p u n", u=2), ALU.add)
                    link_.then_inc(b_qkvev, 1)
                    dve.wait_ge(b_qkvev, at(b, NT, t + 1))
                    t1 = th[0][:, :].rearrange("p (u e j) -> p u e j", u=2, e=2)
                    t2 = th[1][:, :].rearrange("p (u e j) -> p u e j", u=2, e=2)
                    rot = qk[:, :, 0:P].rearrange("p u (e j) -> p u e j", e=2)
                    cb = c1r[:, 0, t].rearrange("p (o w j) -> p o w j", o=1, w=1).broadcast_to([P, 2, 2, 64])
                    sn = c1r[:, 1, t].rearrange("p (o j) -> p o j", o=1).broadcast_to([P, 2, 64])
                    nc.vector.tensor_tensor(t1, rot, cb, ALU.mult)
                    nc.vector.scalar_tensor_tensor(out=t2[:, :, 0, :], in0=rot[:, :, 1, :], scalar=-1.0, in1=sn, op0=ALU.mult, op1=ALU.mult)
                    lnk(b, nc.vector.tensor_tensor(t2[:, :, 1, :], rot[:, :, 0, :], sn, ALU.mult))
                    lnk(b, nc.vector.tensor_tensor(rot, t1, t2, ALU.add))
                    nc.vector.tensor_tensor_reduce(th[0][:, :], qk[:, 1, :], qk[:, 1, :], 1.0, 0.0, ALU.mult, ALU.add,
                                                   ssq[:, t:t + 1]).then_inc(b_ssq, 1)
                dve.wait_ge(b_ssq, at(b, NT, NT))
                nc.vector.tensor_scalar(ssm[:, :], ssq[:, :], NORM_EPS2, None, ALU.max).then_inc(b_ssm, 1)
                dve.wait_ge(b_krn, at(b, 1, 1))
                for t in range(NT):
                    nc.vector.scalar_tensor_tensor(out=kv[:, t], in0=qk_all[:, t, 1, :], scalar=krn[:, t:t + 1], in1=kv[:, t],
                                                   op0=ALU.mult, op1=ALU.mult).then_inc(b_kv, 1)
                yield
                dve.wait_ge(b_A, at(b, 1, 1))
                for t in range(NT):
                    nc.vector.tensor_tensor(qk_all[:, t, 0, :], bY[:, 0:D], qk_all[:, t, 0, :], ALU.mult).then_inc(b_y, 1)
                yield
                split_l(bTB[:, :], bhT_hi[:, :], bhT_lo[:, :], b_hhi, at(b, NLN + 1, 3), b_hlo)
                yield
                dve.wait_ge(b_attn, at(b, 1, 1))
                dve.wait_ge(b_res, at(b, 1, 1))
                lnk(b, nc.vector.tensor_tensor(xB[:, :], bY[:, :], xB[:, :], ALU.add))
                norm_b(b, 2)
                yield
                split_l(bTB[:, :], bhT_hi[:, :], bhT_lo[:, :], b_hhi, at(b, NLN + 1, 4), b_hlo)
                yield
                for t in range(NT):
                    for gi in groups(b, t, FGROUPS, NT * GROUPS, False):
                        for q in range(FQ):
                            if down_after(FGROUPS, q, FFN_HID) == gi:
                                down(b, NT * TQ + t * FQ + q, P * len(chunks_of(FFN_HID, q)))
                        yield
                    dve.wait_ge(b_down, at(b, NQ, NT * TQ + (t + 1) * FQ))
                    nc.vector.scalar_tensor_tensor(out=xB_t[:, t, :], in0=bY[:, 0:D], scalar=0.5, in1=xB_t[:, t, :],
                                                   op0=ALU.mult, op1=ALU.add).then_inc(b_fin, 1)
                    yield
                links["b_total"] = links["b"]


            run(dve, stream_a, stream_b)
            assert links["a"] == A_LINKS and links["b"] == B_LINKS, links

        @block.tensor
        def _(pe):
            pe.wait_ge(consts_in, 16 * 6)
            pe.wait_ge(setup_pool, 4)
            pe.wait_ge(abs_sum, 3)
            nc.tensor.matmul(bY[:, 0:3], ones[:, :], asum[:, :], start=True, stop=True).then_inc(abs_total, 1)
            pe.wait_ge(split_lo, PIECES + 1)
            pe.wait_ge(tern_done, 2 * KD + 1)

            def exact(ps, hi, lo, at_, width, a, b_, kn, start=True, stop=True):
                for k in range(kn):
                    nc.tensor.matmul(ps, hi(k), W(w_hi, at_, k, width, a, b_), start=start and k == 0, stop=False)
                    nc.tensor.matmul(ps, hi(k), W(w_lo, at_, k, width, a, b_), start=False, stop=False)
                    ins = nc.tensor.matmul(ps, lo(k), W(w_hi, at_, k, width, a, b_), start=False, stop=stop and k == kn - 1)
                return ins

            def tr(dst, src, s_done, last):
                ins = nc.tensor.transpose(dst, src, ident[:, :])
                if last:
                    ins.then_inc(s_done, 1)

            def hT(buf, t):
                return lambda k: buf[:, (t * KD + k) * P:(t * KD + k + 1) * P]

            def stream_a(b):
                for t in range(NT):
                    pe.wait_ge(a_h_r, at(b, NT, t + 1))
                    for k in range(KD):
                        tr(bPT[:, (t * KD + k) * P:(t * KD + k + 1) * P], hA_t[:, t, k * P:(k + 1) * P], a_hps, t == NT - 1 and k == KD - 1)
                yield
                pe.wait_ge(a_hlo, at(b, 1, 1))
                for t in range(NT):
                    exact(bS[t][:, :], hT(ahT_hi, t), hT(ahT_lo, t), O_QKV, D + 2 * P, 0, D + 2 * P, KD).then_inc(a_qkv, 1)
                yield
                for t in range(NT):
                    pe.wait_ge(a_stlo, at(b, NT, t + 1))
                    for j in range(3):
                        n = 3 * t + j
                        dst = (bPT, bC)[n % 2]
                        if n >= 2:
                            pe.wait_ge((a_stev_act, a_stev_dve)[n % 2], at(b, 3, n // 2))
                        for i in range(4):
                            src = qs if j < 2 else ks
                            c = (4 * j if j < 2 else 0) + i
                            tr(dst[:, i * P:(i + 1) * P], src[:, c * P:(c + 1) * P].bitcast(F32), a_stT, i == 3)
                    yield
                pe.wait_ge(a_stev_act, at(b, 3, 3))
                pe.wait_ge(a_stev_dve, at(b, 3, 3))
                pe.wait_ge(a_zlo, at(b, NT, NT))
                for h in range(HEADS + 2):
                    if h < HEADS:
                        blk, half = h // 2, h % 2
                        if h >= 2:
                            pe.wait_ge(a_exp, at(b, HEADS, h - 1))
                        for st in range(NT):
                            ins = nc.tensor.matmul(bS[half][:, st * S:(st + 1) * S],
                                                   qT[64 * half:64 * half + 64, blk * S + st * P:blk * S + (st + 1) * P],
                                                   kT[64 * half:64 * half + 64, (blk // 2) * S:(blk // 2 + 1) * S],
                                                   start=True, stop=True)
                        ins.then_inc(a_score, 1)
                    if 1 <= h <= HEADS:
                        pe.wait_ge(a_prob, at(b, HEADS, h))
                        if h >= 2:
                            pe.wait_ge(a_plo, at(b, HEADS, h - 1))
                        for tc in range(NT):
                            for st in range(NT):
                                tr(bPT[:, (tc * NT + st) * P:(tc * NT + st + 1) * P],
                                   pr[(h - 1) % 2][:, st * S + tc * P:st * S + (tc + 1) * P], a_pps, tc == NT - 1 and st == NT - 1)
                    if h >= 2:
                        n = h - 2
                        blk, half = n // 2, n % 2
                        head = ((blk // 2) * 2 + half) * G + blk % 2
                        first, last = n % 8 == 0, n % 8 == 7
                        pe.wait_ge(a_plo, at(b, HEADS, n + 1))
                        dst = bC[:, (n // 8) * S:(n // 8 + 1) * S]
                        for tc in range(NT):
                            a = tc * ZCOLS + zwindow(head)
                            hi = pT_hi[n % 2][:, tc * S:(tc + 1) * S]
                            lo = pT_lo[n % 2][:, tc * S:(tc + 1) * S]
                            nc.tensor.matmul(dst, z_hi[:, a:a + P], hi, start=first and tc == 0, stop=False)
                            nc.tensor.matmul(dst, z_lo[:, a:a + P], hi, start=False, stop=False)
                            ins = nc.tensor.matmul(dst, z_hi[:, a:a + P], lo, start=False, stop=last and tc == NT - 1)
                        ins.then_inc(a_pv, 1)
                    yield
                pe.wait_ge(a_clo, at(b, 1, 1))
                for t in range(NT):
                    def cT(buf):
                        return lambda k: buf[:, k * S + t * P:k * S + (t + 1) * P]
                    ins = exact(bS[0][:, t * D:(t + 1) * D], cT(cT_hi), cT(cT_lo), O_WO, D, 0, D, KD)
                ins.then_inc(a_wo, 1)
                yield

            def norm_T(b, n, src):
                for t in range(NT):
                    if n != 2:
                        pe.wait_ge(b_h_r, at(b, NLN * NT, (n - (n > 2)) * NT + t + 1))
                    else:
                        pe.wait_ge(b_y, at(b, NT, t + 1))
                    for k in range(KD):
                        tr(bTB[:, (t * KD + k) * P:(t * KD + k + 1) * P], src(t)[:, k * P:(k + 1) * P], b_hps, t == NT - 1 and k == KD - 1)

            def down_T(b, m, q, n_hid, need):
                pe.wait_ge(b_hid, need)
                if m >= 1:
                    pe.wait_ge(b_tlo, at(b, NQ, m))
                cs = chunks_of(n_hid, q)
                for i, (c, rows) in enumerate(cs):
                    tr(bTB[0:rows, i * P:(i + 1) * P], hid[:, c * P:c * P + rows], b_tps, i == len(cs) - 1)

            def down_mm(b, m, t, q, n_hid, ternary):
                cs = chunks_of(n_hid, q)
                n_c = -(-n_hid // P)
                pe.wait_ge(b_tlo, at(b, NQ, m + 1))
                for i, (c, rows) in enumerate(cs):
                    hi = hdT_hi[m % 2][0:rows, i * P:(i + 1) * P]
                    lo = hdT_lo[m % 2][0:rows, i * P:(i + 1) * P]
                    y = bY[:, 0:D]
                    if ternary:
                        w = w3q[0:rows, c * D:(c + 1) * D]
                        nc.tensor.matmul(y, hi, w, start=c == 0, stop=False)
                        ins = nc.tensor.matmul(y, lo, w, start=False, stop=c == n_c - 1)
                    else:
                        wh, wl = (p[0:rows, O_W2 + c * D:O_W2 + (c + 1) * D] for p in (w_hi, w_lo))
                        nc.tensor.matmul(y, hi, wh, start=c == 0, stop=False)
                        nc.tensor.matmul(y, hi, wl, start=False, stop=False)
                        ins = nc.tensor.matmul(y, lo, wh, start=False, stop=c == n_c - 1)
                ins.then_inc(b_down, 1)

            def mlp(b, t, n, n_hid, nq, g0, q0, ternary):
                for gi in range(n):
                    m = g0 + t * n + gi
                    if m >= 2:
                        pe.wait_ge(b_hid, at(b, NG, m - 1))
                    dst = bG[m % 2]
                    if ternary:
                        for k in range(KD):
                            w = w12q[:, (k * FGROUPS + gi) * PAIR:(k * FGROUPS + gi + 1) * PAIR]
                            nc.tensor.matmul(dst[:, 0:PAIR], hT(bhT_hi, t)(k), w, start=k == 0, stop=False)
                            ins = nc.tensor.matmul(dst[:, 0:PAIR], hT(bhT_lo, t)(k), w, start=False, stop=k == KD - 1)
                    else:
                        a = group_start(gi)
                        w = PAIR + (EXPERTS if gi == 0 else 0)
                        ins = exact(dst[:, 0:w], hT(bhT_hi, t), hT(bhT_lo, t), O_W13, W13, a, a + w, KD)
                    ins.then_inc(b_grp, 1)
                    for q in range(nq):
                        if down_after(n, q, n_hid) == gi:
                            need = min(-(-(4 * q + 4) * P // INTER), n)
                            down_T(b, q0 + t * nq + q, q, n_hid, at(b, NG, g0 + t * n + need))
                            if q == 0 and t > 0:
                                pe.wait_ge(b_fin if ternary else b_res1, at(b, NT, t))
                            down_mm(b, q0 + t * nq + q, t, q, n_hid, ternary)
                    yield

            def stream_b(b):
                norm_T(b, 0, lambda t: hB_t[:, t, :])
                yield
                pe.wait_ge(b_hlo, at(b, NLN + 1, 1))
                for t in range(NT):
                    yield from mlp(b, t, GROUPS, HID, TQ, 0, 0, False)
                norm_T(b, 1, lambda t: hB_t[:, t, :])
                yield
                pe.wait_ge(b_hlo, at(b, NLN + 1, 2))
                for t in range(NT):
                    if t > 0:
                        pe.wait_ge(b_qkvev, at(b, NT, t))
                    exact(bG[0][:, :], hT(bhT_hi, t), hT(bhT_lo, t), O_WIN, 3 * D, 0, 2 * D, KD)
                    exact(bG[1][:, 0:D], hT(bhT_hi, t), hT(bhT_lo, t), O_WIN, 3 * D, 2 * D, 3 * D, KD).then_inc(b_qkv, 1)
                yield
                for t in range(NT):
                    pe.wait_ge(b_kv, at(b, NT, t + 1))
                    ins = nc.tensor.matmul(bY[:, 0:D], ones[:, :], hid[:, NT * 2 * D + t * D:NT * 2 * D + (t + 1) * D],
                                           start=t == 0, stop=t == NT - 1)
                ins.then_inc(b_A, 1)
                yield
                norm_T(b, 2, lambda t: hid[:, t * 2 * D:t * 2 * D + D])
                yield
                pe.wait_ge(b_hlo, at(b, NLN + 1, 3))
                for t in range(NT):
                    ins = exact(bY[:, t * D:(t + 1) * D], hT(bhT_hi, t), hT(bhT_lo, t), O_WOUT, D, 0, D, KD)
                ins.then_inc(b_attn, 1)
                yield
                norm_T(b, 3, lambda t: hB_t[:, t, :])
                yield
                pe.wait_ge(b_hlo, at(b, NLN + 1, 4))
                for t in range(NT):
                    yield from mlp(b, t, FGROUPS, FFN_HID, FQ, NT * GROUPS, NT * TQ, True)

            run(pe, stream_a, stream_b)


def fold(w):
    rows, cols = w.shape
    n = -(-rows // P)
    full = np.zeros((n * P, cols), w.dtype)
    full[:rows] = w
    return full.reshape(n, P, cols).transpose(1, 0, 2).reshape(P, n * cols)


def pack_weights(i):
    wq = i["L0_attn_W_Q"].T.reshape(D, DH, 4, 2, G).transpose(0, 2, 4, 3, 1).reshape(D, D)
    wk = i["L0_attn_W_K"].T.reshape(D, DH, KV).transpose(0, 2, 1).reshape(D, P)
    wv = i["L0_attn_W_V"].T.reshape(D, DH, KV).transpose(0, 2, 1).reshape(D, P)
    cols = []
    for s in range(SHARED):
        r = slice(s * INTER, (s + 1) * INTER)
        cols += [i["L0_ffn_sw1"][r].T, i["L0_ffn_sw3"][r].T]
        if s == 0:
            cols.append(i["L0_ffn_gate_w"].T)
    for e in range(EXPERTS):
        cols += [i["L0_ffn_W1"][e], i["L0_ffn_W3"][e]]
    w2 = np.concatenate([i["L0_ffn_sw2"].T, i["L0_ffn_W2"].reshape(EXPERTS * INTER, D)], 0)
    order = channel_order()
    win = i["L1_attn_W_in"].reshape(3, D, D)[:, order, :].reshape(3 * D, D).T
    wout = i["L1_attn_W_out"].T[order]
    return np.ascontiguousarray(np.concatenate(
        [fold(np.concatenate([wq, wk, wv], 1)), fold(i["L0_attn_W_O"].T), fold(np.concatenate(cols, 1)), fold(w2),
         fold(win), fold(wout)], 1))


def channel_order():
    return np.concatenate([np.arange(0, D // 2, 2), np.arange(1, D // 2, 2), np.arange(D // 2, D)])


def rope_tables():
    f = np.float32
    pos = np.arange(S, dtype=f).reshape(NT, P)
    inv0 = f(1.0) / f(10000.0) ** (np.arange(0, DH // 2, dtype=f) * f(2.0) / f(DH))
    ang0 = pos[:, :, None] * inv0
    scale = np.concatenate([np.full(HEADS, 1.0 / np.sqrt(D)), np.ones(KV)]).astype(f)
    r0 = np.stack([np.cos(ang0), np.sin(ang0)])[:, :, :, None, :] * scale[:, None]
    rot = D // 2
    inv1 = f(1.0) / f(10000.0) ** (np.arange(0, rot, 2, dtype=f) / f(rot))
    ang1 = pos[:, :, None] * inv1
    r1 = np.stack([np.cos(ang1), np.sin(ang1)])
    return (np.ascontiguousarray(r0.transpose(2, 0, 1, 3, 4).reshape(P, -1).astype(f)),
            np.ascontiguousarray(r1.transpose(2, 0, 1, 3).reshape(P, -1).astype(f)))


def kernel(**inputs):
    import concourse.bacc as _bacc
    from concourse.bass_utils import run_bass_kernel_spmd as _run

    i = {k: np.asarray(v) for k, v in inputs.items()}
    r0, r1 = rope_tables()
    order = channel_order()
    arrays = {
        "x": np.ascontiguousarray(i["L0_attn_x"]),
        "wpack": pack_weights(i),
        "tern1": np.ascontiguousarray(fold(i["L1_ffn_w1"].T)),
        "tern2": np.ascontiguousarray(fold(i["L1_ffn_w2"].T)),
        "tern3": np.ascontiguousarray(fold(i["L1_ffn_w3"].T)),
        "rbias": np.ascontiguousarray(i["L0_ffn_router_bias"]),
        "b_in": np.ascontiguousarray(i["L1_attn_b_in"].reshape(3, D)[:, order].reshape(-1)),
        "b_out": np.ascontiguousarray(i["L1_attn_b_out"]),
        "rope0": r0,
        "rope1": r1,
        "eye": np.eye(P, dtype=np.float32),
    }
    nc = _bacc.Bacc("TRN2", target_bir_lowering=False, num_devices=1)
    args = [nc.dram_tensor(f"in_{n}", a.shape, mybir.dt.from_np(a.dtype), kind="ExternalInput").ap()
            for n, a in arrays.items()]
    out = nc.dram_tensor("out_y", (BATCHES, S, D), F32, kind="ExternalOutput").ap()
    build(nc, *args, out)
    r = _run(nc, [{f"in_{n}": a for n, a in arrays.items()}], core_ids=[0])
    return r.results[0]["out_y"]
```

```python
from contextlib import ExitStack

import numpy as np

import concourse.bass as bass
from concourse import mybir

F32 = mybir.dt.float32
F32R = mybir.dt.float32r
U32 = mybir.dt.uint32
ALU = mybir.AluOpType
ACT = mybir.ActivationFunctionType
AX = mybir.AxisListType

P = 128
D = 256
KD = D // P
BATCHES = 8
S = 256
NT = S // P
HEADS, KV, G, DH = 16, 8, 2, 16
EXPERTS, INTER, SHARED = 8, 176, 2
GROUPS = SHARED + EXPERTS
HID = GROUPS * INTER
CHUNKS = -(-HID // P)
FFN_HID = 704
FGROUPS = FFN_HID // INTER
FCHUNKS = -(-FFN_HID // P)
PAIR = 2 * INTER
W13 = GROUPS * PAIR + EXPERTS
LN_EPS = 1e-5
NORM_EPS2 = 1e-24
QUANT_EPS = 1e-8

O_QKV = 0
O_WO = O_QKV + KD * (D + 2 * P)
O_W13 = O_WO + KD * D
O_W2 = O_W13 + KD * W13
O_WIN = O_W2 + CHUNKS * D
O_WOUT = O_WIN + KD * 3 * D
WCOLS = O_WOUT + KD * D
PIECES = 8
PW = -(-(WCOLS - O_W13) // PIECES)
WCUTS = [0, O_W13] + [min(O_W13 + PW * (n + 1), WCOLS) for n in range(PIECES)]
TW = KD * FFN_HID
STAGE = max(PW, FCHUNKS * D, TW, O_W13)
SLOTS = 3

ZSTEP = P
ZHALF = 3 * P + 2 * DH
ZCOLS = 2 * ZHALF + DH


def zwindow(head):
    kv = head // G
    return (kv // 4) * ZHALF + DH + ZSTEP * (kv % 4) - DH * (head % 8)


def group_start(gi):
    return gi * PAIR + (EXPERTS if gi else 0)


def build(nc, x, wpack, tern1, tern2, tern3, rbias, b_in, b_out, rope0, rope1, eye, out):
    ctx = ExitStack()
    with ctx:
        def sb(name, cols, dt=F32, where=ctx):
            return where.enter_context(nc.sbuf_tensor(name, [P, cols], dt))

        def sem(name):
            return ctx.enter_context(nc.semaphore(name))

        w_hi = sb("w_hi", WCOLS, F32R)
        w_lo = sb("w_lo", WCOLS, F32R)
        w12q = sb("w12q", 2 * TW, F32R)
        w3q = sb("w3q", FCHUNKS * D, F32R)
        ident = sb("ident", P)
        ones = sb("ones", P)
        cos0 = sb("rope0_sb", 2 * NT * 192)
        cs1 = sb("rope1_sb", 2 * NT * 64)
        bin_sb = sb("bin_sb", 3 * D)
        bout_sb = sb("bout_sb", D)
        rb_sb = sb("rb_sb", EXPERTS)
        mhalf = sb("mhalf", NT)
        epst = sb("epst", NT)
        iot = sb("iot", EXPERTS)
        fence = sb("fence", 2)
        a_st = sb("a_st", NT * 6)
        a_mv = sb("a_mv", NT * 2)
        a_ve = sb("a_ve", NT)
        a_rstd = sb("a_rstd", NT)
        nmax = [sb(f"nmax{i}", NT) for i in range(2)]
        rsum = [sb(f"rsum{i}", NT) for i in range(2)]
        rrec = [sb(f"rrec{i}", NT) for i in range(2)]
        b_st = sb("b_st", NT * 6)
        b_mv = sb("b_mv", NT * 2)
        b_ve = sb("b_ve", NT)
        b_rstd = sb("b_rstd", NT)
        r_e = sb("r_e", EXPERTS)
        r_sc = sb("r_sc", EXPERTS)
        r_sel = sb("r_sel", EXPERTS)
        r_top = sb("r_top", 8)
        r_idx = sb("r_idx", 8, U32)
        r_idf = sb("r_idf", 8)
        r_m = sb("r_m", EXPERTS)
        r_sum = sb("r_sum", 4)
        gate = sb("gate", EXPERTS)
        ssq = sb("ssq", NT)
        ssm = sb("ssm", NT)
        krn = sb("krn", NT)
        asum = sb("asum", 3)
        thr = sb("thr", 3 * 2)

        xA = sb("xA", NT * D)
        qT = sb("qT", 8 * S, F32R)
        kT = sb("kT", 4 * S, F32R)
        z_hi = sb("z_hi", NT * ZCOLS, F32R)
        z_lo = sb("z_lo", NT * ZCOLS, F32R)
        with ExitStack() as early:
            ahT_hi = sb("ahT_hi", NT * D, F32R, early)
            ahT_lo = sb("ahT_lo", NT * D, F32R, early)
            hA = sb("hA", NT * D, F32, early)
            t1A = sb("t1A", 384, F32, early)
            t2A = sb("t2A", 384, F32, early)
            qs = sb("qs", 1024, F32R, early)
            ks = sb("ks", 512, F32R, early)
        cT_hi = sb("cT_hi", NT * D, F32R)
        cT_lo = sb("cT_lo", NT * D, F32R)
        pr = [sb(f"pr{i}", NT * S) for i in range(2)]
        pT_hi = [sb(f"pT_hi{i}", NT * S, F32R) for i in range(2)]
        pT_lo = [sb(f"pT_lo{i}", NT * S, F32R) for i in range(2)]

        with ExitStack() as prep:
            stage = [sb(f"stage{i}", STAGE, F32, prep) for i in range(SLOTS)]
        xB = sb("xB", NT * D)
        hB = sb("hB", NT * D)
        bhT_hi = sb("bhT_hi", NT * D, F32R)
        bhT_lo = sb("bhT_lo", NT * D, F32R)
        hid = sb("hid", HID)
        th = [sb(f"th{i}", INTER) for i in range(2)]
        up = [sb(f"up{i}", INTER) for i in range(2)]
        with ExitStack() as attn1:
            rt1, rt2, sq = (sb(n, 2 * P, F32, attn1) for n in ("rt1", "rt2", "sq"))
        hdT_hi = [sb(f"hdT_hi{i}", 512, F32R) for i in range(2)]
        hdT_lo = [sb(f"hdT_lo{i}", 512, F32R) for i in range(2)]

        bank = [ctx.enter_context(nc.psum_tensor(f"bank{i}", [P, 512], F32)) for i in range(8)]
        bS, bPT, bC = bank[0:2], bank[2], bank[3]
        bG, bTB, bY = bank[4:6], bank[6], bank[7]

        def v2(t, a):
            return t[:, :].rearrange("p (a n) -> p a n", a=a)

        x_t, xA_t, xB_t, hA_t, hB_t = (v2(t, NT) for t in (xA, xA, xB, hA, hB))
        cosr = cos0[:, :].rearrange("p (f t h j) -> p f t h j", f=2, t=NT, j=8)
        c1r = cs1[:, :].rearrange("p (f t j) -> p f t j", f=2, t=NT)
        x_b = x.rearrange("b (t p) d -> b p t d", p=P)
        out_b = out.rearrange("b (t p) d -> b p t d", p=P)

        def W(part, at, k, width, a, b):
            return part[:, at + k * width + a:at + k * width + b]

        block = ctx.enter_context(nc.Block())

        stage_in = [sem(f"stage_in{i}") for i in range(SLOTS)]
        consts_in, x_in, xB_free = sem("consts_in"), sem("x_in"), sem("xB_free")
        setup_pool, zeros_ready = sem("setup_pool"), sem("zeros_ready")
        split_hi, split_lo = sem("split_hi"), sem("split_lo")
        abs_sum, abs_total, tern_done, quant_chain = sem("abs_sum"), sem("abs_total"), sem("tern_done"), sem("quant_chain")
        a_chain, a_mv_r, a_ve_r, a_rstd_r, a_h_r = (sem(f"a_{n}") for n in ("chain", "mv_r", "ve_r", "rstd_r", "h_r"))
        a_hps, a_hhi, a_hlo, a_pool = sem("a_hps"), sem("a_hhi"), sem("a_hlo"), sem("a_pool")
        a_qkv, a_raw, a_rope, a_zhi, a_zlo, a_sthi, a_stlo = (
            sem(f"a_{n}") for n in ("qkv", "raw", "rope", "zhi", "zlo", "sthi", "stlo"))
        a_stT, a_stev_act, a_stev_dve = sem("a_stT"), sem("a_stev_act"), sem("a_stev_dve")
        a_score, a_nmax, a_exp, a_rrec, a_prob = (sem(f"a_{n}") for n in ("score", "nmax", "exp", "rrec", "prob"))
        a_pps, a_phi, a_plo, a_pv = (sem(f"a_{n}") for n in ("pps", "phi", "plo", "pv"))
        a_chi, a_clo, a_wo, a_xmid = (sem(f"a_{n}") for n in ("chi", "clo", "wo", "xmid"))
        b_chain, b_xcopy, b_mv_r, b_ve_r, b_rstd_r, b_h_r = (sem(f"b_{n}") for n in ("chain", "xcopy", "mv_r", "ve_r", "rstd_r", "h_r"))
        b_hps, b_hhi, b_hlo = sem("b_hps"), sem("b_hhi"), sem("b_hlo")
        b_grp, b_route, b_gate, b_th, b_up, b_silu, b_hid = (sem(f"b_{n}") for n in ("grp", "route", "gate", "th", "up", "silu", "hid"))
        b_tps, b_thi, b_tlo, b_down, b_res1 = (sem(f"b_{n}") for n in ("tps", "thi", "tlo", "down", "res1"))
        b_qkv, b_qkvev, b_pool, b_rope, b_ssq, b_ssm, b_krn, b_kv, b_A, b_y = (
            sem(f"b_{n}") for n in ("qkv", "qkvev", "pool", "rope", "ssq", "ssm", "krn", "kv", "A", "y"))
        b_attn, b_hb, b_res, b_res2, b_fin = (sem(f"b_{n}") for n in ("attn", "hb", "res", "res2", "fin"))

        def at(b, per, k):
            return b * per + k

        NLN = 3
        NM, NF = NT * GROUPS, NT * FGROUPS
        NG = NM + NF
        TQ, FQ = -(-CHUNKS // 4), -(-FCHUNKS // 4)
        NQ = NT * (TQ + FQ)

        def chunks_of(n_hid, q):
            return [(c, min(P, n_hid - c * P)) for c in range(4 * q, min(4 * q + 4, -(-n_hid // P)))]

        def groups_for(n_hid, q):
            return min(-(-(4 * q + 4) * P // INTER), n_hid // INTER)

        def sets_at(n_hid, slot, lag):
            n, nq = n_hid // INTER, -(-(-(-n_hid // P)) // 4)
            return [(t, q) for t in range(NT) for q in range(nq) if t * n + groups_for(n_hid, q) + lag == slot]

        MLP_SLOTS = NM + 3
        FFN_SLOTS = NF + 3

        A_SLOTS = 6 + HEADS + 3 + 2
        B_SLOTS = 2 + MLP_SLOTS + 9 + FFN_SLOTS
        PREP_SLOTS = PIECES + 4
        A_BEHIND = a_schedule(B_SLOTS, A_SLOTS)

        def together(first, second, n_first, n_second, behind):
            done = 0
            for i in range(n_first):
                next(first)
                for _ in range(behind[i]):
                    next(second)
                    done += 1
            assert done == n_second and next(first, None) is None and next(second, None) is None

        def program(eng, prepare, stream_a, stream_b):
            together(stream_a(0), prepare(), A_SLOTS, PREP_SLOTS, [1 if i < PREP_SLOTS else 0 for i in range(A_SLOTS)])
            with eng.Fori(0, BATCHES - 1) as b:
                together(stream_b(b), stream_a(b + 1), B_SLOTS, A_SLOTS, A_BEHIND)
            for _ in stream_b(BATCHES - 1):
                pass

        def vview(ps, u):
            a = D + P + u * 4 * DH
            return ps[:, a:a + 4 * DH].rearrange("p (v d) -> p v d", d=DH)

        def zview(z, t, u):
            first, step = 1 + u * (ZHALF // DH), ZSTEP // DH
            return z[:, t * ZCOLS:(t + 1) * ZCOLS].rearrange("p (c d) -> p c d", d=DH)[:, first:first + 3 * step + 1:step, :]

        def stack_dst(j, t):
            dst = qT if j < 2 else kT
            a = 4 * j if j < 2 else 0
            return dst[:, :].rearrange("p (k n) -> p k n", n=S)[:, a:a + 4, t * P:(t + 1) * P]

        q4 = qs[:, :].rearrange("p (h s d) -> p h s d", s=4, d=DH)
        k4 = ks[:, :].rearrange("p (h s d) -> p h s d", s=4, d=DH)
        q1 = t1A[:, 0:D].rearrange("p (h o d) -> p h o d", o=1, d=DH).broadcast_to([P, HEADS, 2, DH])
        k1 = t1A[:, D:D + P].rearrange("p (h o d) -> p h o d", o=1, d=DH).broadcast_to([P, KV, 2, DH])
        raw = hA[:, 0:384]
        qk_all = hid[:, 0:NT * 2 * D].rearrange("p (t u n) -> p t u n", t=NT, u=2)
        kv = hid[:, NT * 2 * D:NT * 3 * D].rearrange("p (t n) -> p t n", t=NT)

        @block.sync
        def _(sp):
            sp.dma_start(xA_t, x_b[0]).then_inc(x_in, 16)
            sp.dma_start(stage[0][:, 0:WCUTS[1]], wpack[:, 0:WCUTS[1]]).then_inc(stage_in[0], 16)
            for t, src in ((ident, eye), (cos0, rope0), (cs1, rope1)):
                sp.dma_start(t[:, :], src).then_inc(consts_in, 16)
            for t, src, n in ((bin_sb, b_in, 3 * D), (bout_sb, b_out, D), (rb_sb, rbias, EXPERTS)):
                sp.dma_start(t[:, :], src.rearrange("(a n) -> a n", a=1).broadcast_to([P, n])).then_inc(consts_in, 16)
            for n in range(1, PIECES + 1):
                if n >= SLOTS:
                    sp.wait_ge(split_lo, n - SLOTS + 1)
                a, b = WCUTS[n], WCUTS[n + 1]
                sp.dma_start(stage[n % SLOTS][:, 0:b - a], wpack[:, a:b]).then_inc(stage_in[n % SLOTS], 16)
            for j, (src, w) in enumerate(((tern1, TW), (tern2, TW), (tern3, FCHUNKS * D))):
                n = PIECES + 1 + j
                sp.wait_ge(split_lo, n - SLOTS + 1)
                sp.dma_start(stage[n % SLOTS][:, 0:w], src).then_inc(stage_in[n % SLOTS], 16)

            def load_x(b):
                sp.wait_ge(b_xcopy, at(b - 1, 1, 1))
                sp.dma_start(xA_t, x_b[b]).then_inc(x_in, 16)

            def store(b):
                sp.wait_ge(b_fin, at(b, NT, NT))
                sp.dma_start(out_b[b], xB_t).then_inc(xB_free, 16)

            with sp.Fori(1, BATCHES) as b:
                load_x(b)
                store(b - 1)
            store(BATCHES - 1)
            sp.wait_ge(xB_free, 16 * (BATCHES + 1))

        @block.gpsimd
        def _(pool):
            nc.gpsimd.memset(ones[:, :], 1.0).then_inc(setup_pool, 1)
            nc.gpsimd.memset(fence[:, 1:2], 0.0).then_inc(xB_free, 16)
            nc.gpsimd.memset(mhalf[:, :], -0.5).then_inc(setup_pool, 1)
            nc.gpsimd.memset(epst[:, :], LN_EPS).then_inc(setup_pool, 1)
            nc.gpsimd.iota(iot[:, :], pattern=[[1, EXPERTS]], base=0, channel_multiplier=0,
                           allow_small_or_imprecise_dtypes=True).then_inc(setup_pool, 1)
            pool.wait_ge(setup_pool, 4)
            pool.wait_ge(consts_in, 16 * 6)

            def prepare():
                for _ in range(PREP_SLOTS):
                    yield

            def rstd(mv, ve, rs, s_mv, s_ve, s_rs, n_mv, n):
                pool.wait_ge(s_mv, n_mv)
                nc.gpsimd.tensor_tensor(ve[:, :], v2(mv, NT)[:, :, 1], epst[:, :], ALU.add).then_inc(s_ve, 1)
                pool.wait_ge(s_ve, n)
                nc.gpsimd.tensor_tensor(rs[:, :], ve[:, :], mhalf[:, :], ALU.pow).then_inc(s_rs, 1)

            def rotate(src, t1, t2, out0, cos, sin, step, s, at_):
                nc.gpsimd.tensor_tensor(t1, src, cos, ALU.mult)
                nc.gpsimd.tensor_tensor(t2[:, :, 0, :], src[:, :, 1, :], sin, ALU.mult)
                nc.gpsimd.tensor_tensor(t2[:, :, 1, :], src[:, :, 0, :], sin, ALU.mult).then_inc(s, 1)
                pool.wait_ge(s, at_)
                nc.gpsimd.tensor_tensor(out0[:, :, 0, :], t1[:, :, 0, :], t2[:, :, 0, :], ALU.subtract)
                return nc.gpsimd.tensor_tensor(out0[:, :, 1, :], t1[:, :, 1, :], t2[:, :, 1, :], ALU.add)

            def rope_a(b, t):
                pool.wait_ge(a_raw, at(b, NT, t + 1))
                t1 = t1A[:, :].rearrange("p (h e j) -> p h e j", e=2, j=8)
                t2 = t2A[:, :].rearrange("p (h e j) -> p h e j", e=2, j=8)
                cosb = cosr[:, 0, t].rearrange("p h (o j) -> p h o j", o=1).broadcast_to([P, 24, 2, 8])
                rotate(raw.rearrange("p (h e j) -> p h e j", e=2, j=8), t1, t2, t1, cosb, cosr[:, 1, t], None,
                       a_pool, at(b, NT, t + 1)).then_inc(a_rope, 1)

            def stack_lo(b, t):
                pool.wait_ge(a_sthi, at(b, NT, t + 1))
                nc.gpsimd.tensor_tensor(q4[:, :, 2:4, :], q1, q4[:, :, 0:2, :].bitcast(F32), ALU.subtract)
                nc.gpsimd.tensor_tensor(k4[:, :, 1:4:2, :], k1, k4[:, :, 0:4:2, :].bitcast(F32), ALU.subtract).then_inc(a_stlo, 1)

            def stream_a(b):
                rstd(a_mv, a_ve, a_rstd, a_mv_r, a_ve_r, a_rstd_r, at(b, NT, NT), at(b, 1, 1))
                yield
                yield
                rope_a(b, 0)
                yield
                stack_lo(b, 0)
                pool.wait_ge(a_stlo, at(b, NT, 1))
                rope_a(b, 1)
                yield
                stack_lo(b, 1)
                yield
                yield
                for i in range(HEADS + 3):
                    if 1 <= i <= HEADS:
                        h = i - 1
                        pool.wait_ge(a_rrec, at(b, HEADS, h + 1))
                        nc.gpsimd.tensor_tensor(v2(pr[h % 2], NT), v2(pr[h % 2], NT),
                                                rrec[h % 2][:, :].rearrange("p (t o) -> p t o", o=1).broadcast_to([P, NT, S]),
                                                ALU.mult).then_inc(a_prob, 1)
                    yield
                yield
                yield

            def norm_b(b, n):
                rstd(b_mv, b_ve, b_rstd, b_mv_r, b_ve_r, b_rstd_r, at(b, NLN * NT, NT * (n + 1)), at(b, NLN, n + 1))

            def stream_b(b):
                norm_b(b, 0)
                yield
                yield
                for s in range(MLP_SLOTS):
                    if s < NM:
                        gi = s % GROUPS
                        pool.wait_ge(b_silu, at(b, NM, s + 1))
                        nc.gpsimd.tensor_tensor(hid[:, gi * INTER:(gi + 1) * INTER], th[s % 2][:, :], up[s % 2][:, :],
                                                ALU.mult).then_inc(b_hid, 1)
                    yield
                norm_b(b, 1)
                yield
                yield
                for t in range(NT):
                    pool.wait_ge(b_qkvev, at(b, NT, t + 1))
                    if t > 0:
                        pool.wait_ge(b_rope, at(b, NT, t))
                    t1 = rt1[:, :].rearrange("p (u e j) -> p u e j", u=2, e=2)
                    t2 = rt2[:, :].rearrange("p (u e j) -> p u e j", u=2, e=2)
                    rot = qk_all[:, t, :, 0:P].rearrange("p u (e j) -> p u e j", e=2)
                    cb = c1r[:, 0, t].rearrange("p (o w j) -> p o w j", o=1, w=1).broadcast_to([P, 2, 2, 64])
                    sn = c1r[:, 1, t].rearrange("p (o j) -> p o j", o=1).broadcast_to([P, 2, 64])
                    rotate(rot, t1, t2, rot, cb, sn, None, b_pool, at(b, NT, t + 1)).then_inc(b_rope, 1)
                    if t == 0:
                        pool.wait_ge(b_hps, at(b, NLN + 1, 2))
                        nc.gpsimd.tensor_tensor(hB_t, hB_t, bout_sb[:, :].rearrange("p (o n) -> p o n", o=1).broadcast_to([P, NT, D]),
                                                ALU.add).then_inc(b_hb, 1)
                    yield
                pool.wait_ge(b_ssm, at(b, 1, 1))
                nc.gpsimd.tensor_tensor(krn[:, :], ssm[:, :], mhalf[:, :], ALU.pow).then_inc(b_krn, 1)
                yield
                pool.wait_ge(b_hb, at(b, 1, 1))
                nc.gpsimd.tensor_tensor(xB[:, :], xB[:, :], hB[:, :], ALU.add).then_inc(b_res, 1)
                yield
                yield
                norm_b(b, 2)
                yield
                yield
                for s in range(FFN_SLOTS):
                    yield

            program(pool, prepare, stream_a, stream_b)

        @block.scalar
        def _(act):
            def prepare():
                for n in range(PREP_SLOTS):
                    if n <= PIECES:
                        a, b = WCUTS[n], WCUTS[n + 1]
                        act.wait_ge(stage_in[n % SLOTS], 16 * (n // SLOTS + 1))
                        nc.scalar.activation(w_hi[:, a:b], stage[n % SLOTS][:, 0:b - a], ACT.Copy).then_inc(split_hi, 1)
                    yield

            def split_h(ps, dst, s_ps, n_ps, s_hi):
                act.wait_ge(s_ps, n_ps)
                nc.scalar.activation(dst, ps, ACT.Copy).then_inc(s_hi, 1)

            def project_a(b, t):
                act.wait_ge(a_qkv, at(b, NT, t + 1))
                for u in range(2):
                    ins = nc.scalar.activation(zview(z_hi, t, u), vview(bS[t], u), ACT.Copy)
                nc.scalar.activation(raw, bS[t][:, 0:384], ACT.Copy).then_inc(a_raw, 1)

            def stack_hi(b, t):
                act.wait_ge(a_rope, at(b, NT, t + 1))
                nc.scalar.activation(q4[:, :, 0:2, :], q1, ACT.Copy)
                nc.scalar.activation(k4[:, :, 0:4:2, :], k1, ACT.Copy).then_inc(a_sthi, 1)

            def stack_copy(b, t):
                for j in range(3):
                    n = 3 * t + j
                    if n % 2 == 0:
                        act.wait_ge(a_stT, at(b, 3 * NT, n + 1))
                        nc.scalar.activation(stack_dst(j, t), v2(bPT, 4), ACT.Copy).then_inc(a_stev_act, 1)

            def stream_a(b):
                yield
                split_h(bPT[:, :], ahT_hi[:, :], a_hps, at(b, 1, 1), a_hhi)
                yield
                project_a(b, 0)
                yield
                stack_hi(b, 0)
                project_a(b, 1)
                yield
                stack_copy(b, 0)
                stack_hi(b, 1)
                yield
                stack_copy(b, 1)
                yield
                for i in range(HEADS + 3):
                    if 2 <= i < HEADS + 2:
                        h = i - 2
                        if h >= 2:
                            act.wait_ge(a_pv, at(b, HEADS, h - 1))
                        split_h(bPT[:, :], pT_hi[h % 2][:, :], a_pps, at(b, HEADS, h + 1), a_phi)
                    if i < HEADS:
                        h = i
                        act.wait_ge(a_nmax, at(b, HEADS, h + 1))
                        for st in range(NT):
                            ins = nc.scalar.activation(pr[h % 2][:, st * S:(st + 1) * S], bS[h % 2][:, st * S:(st + 1) * S], ACT.Exp,
                                                       bias=nmax[h % 2][:, st:st + 1], accum_out=rsum[h % 2][:, st:st + 1])
                        ins.then_inc(a_exp, 1)
                    yield
                split_h(bC[:, :], cT_hi[:, :], a_pv, at(b, HEADS, HEADS), a_chi)
                yield
                yield

            def down(b, m, cols):
                if m >= 2:
                    act.wait_ge(b_down, at(b, NQ, m - 1))
                split_h(bTB[:, 0:cols], hdT_hi[m % 2][:, 0:cols], b_tps, at(b, NQ, m + 1), b_thi)

            def hT_b(b, n):
                split_h(bTB[:, :], bhT_hi[:, :], b_hps, at(b, NLN + 1, n + 1), b_hhi)

            def stream_b(b):
                act.wait_ge(a_xmid, at(b, 1, 1))
                act.wait_ge(xB_free, at(b, 16, 16))
                nc.scalar.activation(xB[:, :], xA[:, :], ACT.Copy).then_inc(b_xcopy, 1)
                yield
                hT_b(b, 0)
                yield
                for s in range(MLP_SLOTS):
                    for t, q in sets_at(HID, s, 1):
                        down(b, t * TQ + q, P * len(chunks_of(HID, q)))
                    if s < NM:
                        gi = s % GROUPS
                        g = bG[s % 2]
                        act.wait_ge(b_grp, at(b, NG, s + 1))
                        if gi == 0:
                            nc.scalar.activation(r_e[:, :], g[:, PAIR:PAIR + EXPERTS], ACT.Exp, scale=-1.0).then_inc(b_route, 1)
                        if s >= 2:
                            act.wait_ge(b_hid, at(b, NG, s - 1))
                        nc.scalar.activation(th[s % 2][:, :], g[:, 0:INTER], ACT.Tanh, scale=0.5)
                        if gi == SHARED:
                            act.wait_ge(b_gate, at(b, NT, s // GROUPS + 1))
                        half = 0.5 if gi < SHARED else gate[:, gi - SHARED:gi - SHARED + 1]
                        nc.scalar.activation(up[s % 2][:, :], g[:, INTER:PAIR], ACT.Copy, scale=half).then_inc(b_th, 1)
                    yield
                yield
                hT_b(b, 1)
                yield
                for _ in range(4):
                    yield
                hT_b(b, 2)
                yield
                yield
                hT_b(b, 3)
                yield
                for s in range(FFN_SLOTS):
                    for t, q in sets_at(FFN_HID, s, 1):
                        down(b, NT * TQ + t * FQ + q, P * len(chunks_of(FFN_HID, q)))
                    if s < NF:
                        act.wait_ge(b_grp, at(b, NG, NM + s + 1))
                        nc.scalar.activation(th[s % 2][:, :], bG[s % 2][:, 0:INTER], ACT.Tanh, scale=0.5).then_inc(b_th, 1)
                    yield

            program(act, prepare, stream_a, stream_b)

        @block.vector
        def _(dve):
            A_LINKS = 1
            B_LINKS = NLN + NT * 11
            links = {"a": 0, "b": 0}
            chain = {"a": a_chain, "b": b_chain}

            def link(s, b, per, ins):
                links[s] += 1
                ins.then_inc(chain[s], 1)
                dve.wait_ge(chain[s], at(b, per, links[s]))

            def hold():
                nc.vector.memset(fence[:, 0:1], 0.0)

            def lnk(b, ins):
                link("b", b, B_LINKS, ins)

            def prepare():
                for n in range(PIECES + 1):
                    a, b = WCUTS[n], WCUTS[n + 1]
                    dve.wait_ge(split_hi, n + 1)
                    nc.vector.tensor_tensor(w_lo[:, a:b], stage[n % SLOTS][:, 0:b - a], w_hi[:, a:b].bitcast(F32),
                                            ALU.subtract).then_inc(split_lo, 1)
                    yield
                for j, w in enumerate((TW, TW, FCHUNKS * D)):
                    n = PIECES + 1 + j
                    dve.wait_ge(stage_in[n % SLOTS], 16 * (n // SLOTS + 1))
                    nc.vector.tensor_reduce(asum[:, j:j + 1], stage[n % SLOTS][:, 0:w], AX.X, ALU.add,
                                            apply_absolute_value=True).then_inc(abs_sum, 1)
                yield
                dve.wait_ge(abs_total, 1)
                nc.vector.tensor_scalar(thr[:, 0:3], bY[:, 0:3], 1.0 / (FFN_HID * D), QUANT_EPS, ALU.mult, ALU.add).then_inc(quant_chain, 1)
                dve.wait_ge(quant_chain, 1)
                nc.vector.tensor_scalar(thr[:, 3:6], thr[:, 0:3], -0.5, None, ALU.mult).then_inc(quant_chain, 1)
                dve.wait_ge(quant_chain, 2)
                nc.vector.tensor_scalar(thr[:, 0:3], thr[:, 0:3], 0.5, None, ALU.mult).then_inc(quant_chain, 1)
                dve.wait_ge(quant_chain, 3)
                yield
                nq = 3
                for j in range(3):
                    src = stage[(PIECES + 1 + j) % SLOTS]
                    for k in range(KD if j < 2 else 1):
                        w = FFN_HID if j < 2 else FCHUNKS * D
                        s = src[:, k * w:(k + 1) * w]
                        if j < 2:
                            s = s.rearrange("p (g n) -> p g n", n=INTER)
                            d = w12q[:, :].rearrange("p (k g u n) -> p k g u n", k=KD, g=FGROUPS, u=2)[:, k, :, j, :]
                        else:
                            d = w3q[:, :]
                        nc.vector.tensor_scalar(d, s, thr[:, 3 + j:4 + j], None, ALU.is_lt).then_inc(quant_chain, 1)
                        nq += 1
                        dve.wait_ge(quant_chain, nq)
                        nc.vector.scalar_tensor_tensor(out=d, in0=s, scalar=thr[:, j:j + 1], in1=d.bitcast(F32), op0=ALU.is_gt,
                                                       op1=ALU.subtract).then_inc(tern_done, 1)
                yield

            def stats(s, b, per, xt, st, mv, s_mv):
                for t in range(NT):
                    ins = nc.vector.bn_stats(st[:, 6 * t:6 * t + 6], xt[:, t, :])
                link(s, b, per, ins)
                hold()
                for t in range(NT):
                    nc.vector.bn_aggr(mv[:, 2 * t:2 * t + 2], st[:, 6 * t:6 * t + 6]).then_inc(s_mv, 1)

            def normalise(xt, ht, mv, rs, s_rs, n, s_h):
                dve.wait_ge(s_rs, n)
                for t in range(NT):
                    nc.vector.tensor_scalar(ht[:, t, :], xt[:, t, :], mv[:, 2 * t:2 * t + 1], rs[:, t:t + 1],
                                            ALU.subtract, ALU.mult).then_inc(s_h, 1)

            def split_l(ps, hi, dst, s_hi, n_hi, s_lo):
                dve.wait_ge(s_hi, n_hi)
                nc.vector.tensor_tensor(dst, ps, hi.bitcast(F32), ALU.subtract).then_inc(s_lo, 1)

            def project_a(b, t):
                dve.wait_ge(a_raw, at(b, NT, t + 1))
                for u in range(2):
                    ins = nc.vector.tensor_tensor(zview(z_lo, t, u), vview(bS[t], u), zview(z_hi, t, u).bitcast(F32), ALU.subtract)
                ins.then_inc(a_zlo, 1)

            def stack_copy(b, t):
                for j in range(3):
                    n = 3 * t + j
                    if n % 2 == 1:
                        dve.wait_ge(a_stT, at(b, 3 * NT, n + 1))
                        nc.vector.tensor_copy(stack_dst(j, t), v2(bC, 4)).then_inc(a_stev_dve, 1)

            def stream_a(b):
                links["a"] = 0
                dve.wait_ge(x_in, at(b, 16, 16))
                stats("a", b, A_LINKS, xA_t, a_st, a_mv, a_mv_r)
                normalise(xA_t, hA_t, a_mv, a_rstd, a_rstd_r, at(b, 1, 1), a_h_r)
                yield
                split_l(bPT[:, :], ahT_hi[:, :], ahT_lo[:, :], a_hhi, at(b, 1, 1), a_hlo)
                yield
                project_a(b, 0)
                yield
                project_a(b, 1)
                yield
                stack_copy(b, 0)
                yield
                stack_copy(b, 1)
                yield
                for i in range(HEADS + 3):
                    if 1 <= i <= HEADS:
                        h = i - 1
                        dve.wait_ge(a_exp, at(b, HEADS, h + 1))
                        nc.vector.reciprocal(rrec[h % 2][:, :], rsum[h % 2][:, :]).then_inc(a_rrec, 1)
                    if 2 <= i < HEADS + 2:
                        h = i - 2
                        split_l(bPT[:, :], pT_hi[h % 2][:, :], pT_lo[h % 2][:, :], a_phi, at(b, HEADS, h + 1), a_plo)
                    if i < HEADS:
                        dve.wait_ge(a_score, at(b, HEADS, i + 1))
                        nc.vector.tensor_reduce(nmax[i % 2][:, :], v2(bS[i % 2], NT), AX.X, ALU.max, negate=True).then_inc(a_nmax, 1)
                    yield
                split_l(bC[:, :], cT_hi[:, :], cT_lo[:, :], a_chi, at(b, 1, 1), a_clo)
                yield
                dve.wait_ge(a_wo, at(b, 1, 1))
                nc.vector.tensor_tensor(xA[:, :], bS[0][:, :], xA[:, :], ALU.add).then_inc(a_xmid, 1)
                yield

            def route(b, t):
                dve.wait_ge(b_route, at(b, NT, t + 1))
                lnk(b, nc.vector.tensor_scalar(r_sc[:, :], r_e[:, :], 1.0, None, ALU.add))
                lnk(b, nc.vector.reciprocal(r_sc[:, :], r_sc[:, :]))
                lnk(b, nc.vector.tensor_tensor(r_sel[:, :], r_sc[:, :], rb_sb[:, :], ALU.add))
                hold()
                lnk(b, nc.vector.max(r_top[:, :], r_sel[:, :]))
                hold()
                lnk(b, nc.vector.max_index(r_idx[:, :], r_top[:, :], r_sel[:, :]))
                lnk(b, nc.vector.tensor_copy(r_idf[:, :], r_idx[:, :]))
                lnk(b, nc.vector.tensor_scalar(r_m[:, :], iot[:, :], r_idf[:, 0:1], None, ALU.is_equal))
                lnk(b, nc.vector.scalar_tensor_tensor(out=r_m[:, :], in0=iot[:, :], scalar=r_idf[:, 1:2], in1=r_m[:, :],
                                                      op0=ALU.is_equal, op1=ALU.add))
                lnk(b, nc.vector.tensor_tensor_reduce(r_m[:, :], r_m[:, :], r_sc[:, :], 1.0, 0.0, ALU.mult, ALU.add, r_sum[:, 0:1]))
                lnk(b, nc.vector.tensor_scalar(r_sum[:, 1:2], r_sum[:, 0:1], 1e-12, None, ALU.max))
                lnk(b, nc.vector.reciprocal(r_sum[:, 2:3], r_sum[:, 1:2]))
                nc.vector.tensor_scalar(gate[:, :], r_m[:, :], r_sum[:, 2:3], 0.5, ALU.mult, ALU.mult).then_inc(b_gate, 1)

            def down(b, m, cols):
                split_l(bTB[:, 0:cols], hdT_hi[m % 2][:, 0:cols], hdT_lo[m % 2][:, 0:cols], b_thi, at(b, NQ, m + 1), b_tlo)

            def norm_b(b, n):
                stats("b", b, B_LINKS, xB_t, b_st, b_mv, b_mv_r)
                normalise(xB_t, hB_t, b_mv, b_rstd, b_rstd_r, at(b, NLN, n + 1), b_h_r)

            def hT_b(b, n):
                split_l(bTB[:, :], bhT_hi[:, :], bhT_lo[:, :], b_hhi, at(b, NLN + 1, n + 1), b_hlo)

            def stream_b(b):
                links["b"] = 0
                dve.wait_ge(b_xcopy, at(b, 1, 1))
                norm_b(b, 0)
                yield
                hT_b(b, 0)
                yield
                for s in range(MLP_SLOTS):
                    for t, q in sets_at(HID, s, 1):
                        down(b, t * TQ + q, P * len(chunks_of(HID, q)))
                    if s < NM:
                        dve.wait_ge(b_th, at(b, NG, s + 1))
                        u = th[s % 2][:, :]
                        nc.vector.scalar_tensor_tensor(out=u, in0=u, scalar=1.0, in1=bG[s % 2][:, 0:INTER], op0=ALU.add,
                                                       op1=ALU.mult).then_inc(b_silu, 1)
                        if s % GROUPS == 0:
                            route(b, s // GROUPS)
                    for t, q in sets_at(HID, s, 2):
                        if q == TQ - 1:
                            dve.wait_ge(b_down, at(b, NQ, (t + 1) * TQ))
                            nc.vector.tensor_tensor(xB_t[:, t, :], bY[:, 0:D], xB_t[:, t, :], ALU.add).then_inc(b_res1, 1)
                    yield
                dve.wait_ge(b_res1, at(b, NT, NT))
                norm_b(b, 1)
                yield
                hT_b(b, 1)
                yield
                for t in range(NT):
                    dve.wait_ge(b_qkv, at(b, NT, t + 1))
                    nc.vector.tensor_tensor(kv[:, t], bG[1][:, 0:D], bin_sb[:, 2 * D:3 * D], ALU.add)
                    nc.vector.tensor_tensor(qk_all[:, t], v2(bG[0], 2), bin_sb[:, 0:2 * D].rearrange("p (u n) -> p u n", u=2),
                                            ALU.add).then_inc(b_qkvev, 1)
                    yield
                for t in range(NT):
                    dve.wait_ge(b_rope, at(b, NT, t + 1))
                    nc.vector.tensor_tensor_reduce(sq[:, :], qk_all[:, t, 1, :], qk_all[:, t, 1, :], 1.0, 0.0, ALU.mult, ALU.add,
                                                   ssq[:, t:t + 1]).then_inc(b_ssq, 1)
                    dve.wait_ge(b_ssq, at(b, NT, t + 1))
                nc.vector.tensor_scalar(ssm[:, :], ssq[:, :], NORM_EPS2, None, ALU.max).then_inc(b_ssm, 1)
                dve.wait_ge(b_krn, at(b, 1, 1))
                for t in range(NT):
                    nc.vector.scalar_tensor_tensor(out=kv[:, t], in0=qk_all[:, t, 1, :], scalar=krn[:, t:t + 1], in1=kv[:, t],
                                                   op0=ALU.mult, op1=ALU.mult).then_inc(b_kv, 1)
                yield
                dve.wait_ge(b_A, at(b, 1, 1))
                for t in range(NT):
                    nc.vector.tensor_tensor(qk_all[:, t, 0, :], bY[:, 0:D], qk_all[:, t, 0, :], ALU.mult).then_inc(b_y, 1)
                yield
                hT_b(b, 2)
                yield
                dve.wait_ge(b_attn, at(b, 1, 1))
                dve.wait_ge(b_res, at(b, 1, 1))
                nc.vector.tensor_tensor(xB[:, :], bY[:, :], xB[:, :], ALU.add).then_inc(b_res2, 1)
                dve.wait_ge(b_res2, at(b, 1, 1))
                norm_b(b, 2)
                yield
                hT_b(b, 3)
                yield
                for s in range(FFN_SLOTS):
                    for t, q in sets_at(FFN_HID, s, 1):
                        down(b, NT * TQ + t * FQ + q, P * len(chunks_of(FFN_HID, q)))
                    if s < NF:
                        f = s % FGROUPS
                        dve.wait_ge(b_th, at(b, NG, NM + s + 1))
                        nc.vector.scalar_tensor_tensor(out=hid[:, f * INTER:(f + 1) * INTER], in0=th[s % 2][:, :], scalar=1.0,
                                                       in1=bG[s % 2][:, INTER:PAIR], op0=ALU.add, op1=ALU.mult).then_inc(b_hid, 1)
                    for t, q in sets_at(FFN_HID, s, 2):
                        if q == FQ - 1:
                            dve.wait_ge(b_down, at(b, NQ, NT * TQ + (t + 1) * FQ))
                            nc.vector.scalar_tensor_tensor(out=xB_t[:, t, :], in0=bY[:, 0:D], scalar=0.5, in1=xB_t[:, t, :],
                                                           op0=ALU.mult, op1=ALU.add).then_inc(b_fin, 1)
                    yield

            nc.vector.memset(z_hi[:, :].bitcast(F32), 0.0).then_inc(zeros_ready, 1)
            nc.vector.memset(z_lo[:, :].bitcast(F32), 0.0).then_inc(zeros_ready, 1)
            dve.wait_ge(zeros_ready, 2)
            program(dve, prepare, stream_a, stream_b)
            assert links["a"] == A_LINKS and links["b"] == B_LINKS, links

        @block.tensor
        def _(pe):
            def prepare():
                for _ in range(PIECES + 2):
                    yield
                pe.wait_ge(abs_sum, 3)
                nc.tensor.matmul(bY[:, 0:3], ones[:, :], asum[:, :], start=True, stop=True).then_inc(abs_total, 1)
                yield
                yield

            def exact(ps, hi, lo, at_, width, a, b_, kn):
                for k in range(kn):
                    nc.tensor.matmul(ps, hi(k), W(w_hi, at_, k, width, a, b_), start=k == 0, stop=False)
                    nc.tensor.matmul(ps, hi(k), W(w_lo, at_, k, width, a, b_), start=False, stop=False)
                    ins = nc.tensor.matmul(ps, lo(k), W(w_hi, at_, k, width, a, b_), start=False, stop=k == kn - 1)
                return ins

            def tr(dst, src, s_done, last):
                ins = nc.tensor.transpose(dst, src, ident[:, :])
                if last:
                    ins.then_inc(s_done, 1)

            def hT(buf, t):
                return lambda k: buf[:, (t * KD + k) * P:(t * KD + k + 1) * P]

            def stacks(b, t):
                pe.wait_ge(a_stlo, at(b, NT, t + 1))
                for j in range(3):
                    n = 3 * t + j
                    dst = (bPT, bC)[n % 2]
                    if n >= 2:
                        pe.wait_ge((a_stev_act, a_stev_dve)[n % 2], at(b, 3, n // 2))
                    for i in range(4):
                        src = qs if j < 2 else ks
                        c = (4 * j if j < 2 else 0) + i
                        tr(dst[:, i * P:(i + 1) * P], src[:, c * P:(c + 1) * P].bitcast(F32), a_stT, i == 3)

            def stream_a(b):
                yield
                for t in range(NT):
                    pe.wait_ge(a_h_r, at(b, NT, t + 1))
                    for k in range(KD):
                        tr(bPT[:, (t * KD + k) * P:(t * KD + k + 1) * P], hA_t[:, t, k * P:(k + 1) * P], a_hps, t == NT - 1 and k == KD - 1)
                yield
                pe.wait_ge(a_hlo, at(b, 1, 1))
                for t in range(NT):
                    exact(bS[t][:, :], hT(ahT_hi, t), hT(ahT_lo, t), O_QKV, D + 2 * P, 0, D + 2 * P, KD).then_inc(a_qkv, 1)
                    yield
                for t in range(NT):
                    stacks(b, t)
                    yield
                pe.wait_ge(a_stev_act, at(b, 3, 3))
                pe.wait_ge(a_stev_dve, at(b, 3, 3))
                pe.wait_ge(a_zlo, at(b, NT, NT))
                for i in range(HEADS + 3):
                    if 2 <= i < HEADS + 2:
                        h = i - 2
                        pe.wait_ge(a_prob, at(b, HEADS, h + 1))
                        if h >= 1:
                            pe.wait_ge(a_plo, at(b, HEADS, h))
                        for tc in range(NT):
                            for st in range(NT):
                                tr(bPT[:, (tc * NT + st) * P:(tc * NT + st + 1) * P],
                                   pr[h % 2][:, st * S + tc * P:st * S + (tc + 1) * P], a_pps, tc == NT - 1 and st == NT - 1)
                    if i >= 3:
                        h = i - 3
                        blk, half = h // 2, h % 2
                        head = ((blk // 2) * 2 + half) * G + blk % 2
                        first, last = h % 8 == 0, h % 8 == 7
                        pe.wait_ge(a_plo, at(b, HEADS, h + 1))
                        dst = bC[:, (h // 8) * S:(h // 8 + 1) * S]
                        for tc in range(NT):
                            a = tc * ZCOLS + zwindow(head)
                            hi = pT_hi[h % 2][:, tc * S:(tc + 1) * S]
                            lo = pT_lo[h % 2][:, tc * S:(tc + 1) * S]
                            nc.tensor.matmul(dst, z_hi[:, a:a + P], hi, start=first and tc == 0, stop=False)
                            nc.tensor.matmul(dst, z_lo[:, a:a + P], hi, start=False, stop=False)
                            ins = nc.tensor.matmul(dst, z_hi[:, a:a + P], lo, start=False, stop=last and tc == NT - 1)
                        ins.then_inc(a_pv, 1)
                    if i < HEADS:
                        h = i
                        blk, half = h // 2, h % 2
                        if h >= 2:
                            pe.wait_ge(a_exp, at(b, HEADS, h - 1))
                        for st in range(NT):
                            ins = nc.tensor.matmul(bS[half][:, st * S:(st + 1) * S],
                                                   qT[64 * half:64 * half + 64, blk * S + st * P:blk * S + (st + 1) * P],
                                                   kT[64 * half:64 * half + 64, (blk // 2) * S:(blk // 2 + 1) * S],
                                                   start=True, stop=True)
                        ins.then_inc(a_score, 1)
                    yield
                yield
                pe.wait_ge(a_clo, at(b, 1, 1))
                for t in range(NT):
                    def cT(buf):
                        return lambda k: buf[:, k * S + t * P:k * S + (t + 1) * P]
                    ins = exact(bS[0][:, t * D:(t + 1) * D], cT(cT_hi), cT(cT_lo), O_WO, D, 0, D, KD)
                ins.then_inc(a_wo, 1)
                yield

            def hT_b(b, n, src, ready, n_ready):
                for t in range(NT):
                    pe.wait_ge(ready, n_ready(t))
                    for k in range(KD):
                        tr(bTB[:, (t * KD + k) * P:(t * KD + k + 1) * P], src(t)[:, k * P:(k + 1) * P], b_hps, t == NT - 1 and k == KD - 1)

            def h_src(t):
                return hB_t[:, t, :]

            def down_T(b, m, q, n_hid, need):
                pe.wait_ge(b_hid, need)
                if m >= 1:
                    pe.wait_ge(b_tlo, at(b, NQ, m))
                cs = chunks_of(n_hid, q)
                for i, (c, rows) in enumerate(cs):
                    tr(bTB[0:rows, i * P:(i + 1) * P], hid[:, c * P:c * P + rows], b_tps, i == len(cs) - 1)

            def down_mm(b, m, q, n_hid, ternary):
                cs = chunks_of(n_hid, q)
                n_c = -(-n_hid // P)
                pe.wait_ge(b_tlo, at(b, NQ, m + 1))
                for i, (c, rows) in enumerate(cs):
                    hi = hdT_hi[m % 2][0:rows, i * P:(i + 1) * P]
                    lo = hdT_lo[m % 2][0:rows, i * P:(i + 1) * P]
                    y = bY[:, 0:D]
                    if ternary:
                        w = w3q[0:rows, c * D:(c + 1) * D]
                        nc.tensor.matmul(y, hi, w, start=c == 0, stop=False)
                        ins = nc.tensor.matmul(y, lo, w, start=False, stop=c == n_c - 1)
                    else:
                        wh, wl = (p[0:rows, O_W2 + c * D:O_W2 + (c + 1) * D] for p in (w_hi, w_lo))
                        nc.tensor.matmul(y, hi, wh, start=c == 0, stop=False)
                        nc.tensor.matmul(y, hi, wl, start=False, stop=False)
                        ins = nc.tensor.matmul(y, lo, wh, start=False, stop=c == n_c - 1)
                ins.then_inc(b_down, 1)

            def mlp(b, n_hid, slots, g0, q0, ternary):
                n, nq = n_hid // INTER, -(-(-(-n_hid // P)) // 4)
                for s in range(slots):
                    for t, q in sets_at(n_hid, s, 1):
                        down_T(b, q0 + t * nq + q, q, n_hid, at(b, NG, g0 + t * n + groups_for(n_hid, q)))
                    for t, q in sets_at(n_hid, s, 2):
                        if q == 0 and t > 0:
                            pe.wait_ge(b_fin if ternary else b_res1, at(b, NT, t))
                        down_mm(b, q0 + t * nq + q, q, n_hid, ternary)
                    if s < NT * n:
                        t, gi = s // n, s % n
                        if s >= 2:
                            if ternary:
                                pe.wait_ge(b_hid, at(b, NG, g0 + s - 1))
                            else:
                                pe.wait_ge(b_silu, at(b, NM, s - 1))
                        dst = bG[s % 2]
                        if ternary:
                            for k in range(KD):
                                w = w12q[:, (k * FGROUPS + gi) * PAIR:(k * FGROUPS + gi + 1) * PAIR]
                                nc.tensor.matmul(dst[:, 0:PAIR], hT(bhT_hi, t)(k), w, start=k == 0, stop=False)
                                ins = nc.tensor.matmul(dst[:, 0:PAIR], hT(bhT_lo, t)(k), w, start=False, stop=k == KD - 1)
                        else:
                            a = group_start(gi)
                            w = PAIR + (EXPERTS if gi == 0 else 0)
                            ins = exact(dst[:, 0:w], hT(bhT_hi, t), hT(bhT_lo, t), O_W13, W13, a, a + w, KD)
                        ins.then_inc(b_grp, 1)
                    yield

            def stream_b(b):
                yield
                hT_b(b, 0, h_src, b_h_r, lambda t: at(b, NLN * NT, t + 1))
                yield
                pe.wait_ge(b_hlo, at(b, NLN + 1, 1))
                yield from mlp(b, HID, MLP_SLOTS, 0, 0, False)
                yield
                hT_b(b, 1, h_src, b_h_r, lambda t: at(b, NLN * NT, NT + t + 1))
                yield
                pe.wait_ge(b_hlo, at(b, NLN + 1, 2))
                for t in range(NT):
                    if t > 0:
                        pe.wait_ge(b_qkvev, at(b, NT, t))
                    exact(bG[0][:, :], hT(bhT_hi, t), hT(bhT_lo, t), O_WIN, 3 * D, 0, 2 * D, KD)
                    exact(bG[1][:, 0:D], hT(bhT_hi, t), hT(bhT_lo, t), O_WIN, 3 * D, 2 * D, 3 * D, KD).then_inc(b_qkv, 1)
                    yield
                yield
                for t in range(NT):
                    pe.wait_ge(b_kv, at(b, NT, t + 1))
                    ins = nc.tensor.matmul(bY[:, 0:D], ones[:, :], kv[:, t], start=t == 0, stop=t == NT - 1)
                ins.then_inc(b_A, 1)
                yield
                hT_b(b, 2, lambda t: qk_all[:, t, 0, :], b_y, lambda t: at(b, NT, t + 1))
                yield
                pe.wait_ge(b_hlo, at(b, NLN + 1, 3))
                for t in range(NT):
                    ins = exact(bY[:, t * D:(t + 1) * D], hT(bhT_hi, t), hT(bhT_lo, t), O_WOUT, D, 0, D, KD)
                ins.then_inc(b_attn, 1)
                yield
                hT_b(b, 3, h_src, b_h_r, lambda t: at(b, NLN * NT, 2 * NT + t + 1))
                yield
                pe.wait_ge(b_hlo, at(b, NLN + 1, 4))
                yield from mlp(b, FFN_HID, FFN_SLOTS, NM, NT * TQ, True)

            pe.wait_ge(consts_in, 16 * 6)
            pe.wait_ge(setup_pool, 4)
            pe.wait_ge(split_lo, 1)
            program(pe, prepare, stream_a, stream_b)


def a_schedule(n_b, n_a):
    first = 1
    marks = [first + i * (n_b - 1 - first) // (n_a - 1) for i in range(n_a)]
    return [marks.count(i) for i in range(n_b)]


def fold(w):
    rows, cols = w.shape
    n = -(-rows // P)
    full = np.zeros((n * P, cols), w.dtype)
    full[:rows] = w
    return full.reshape(n, P, cols).transpose(1, 0, 2).reshape(P, n * cols)


def pack_weights(i):
    wq = i["L0_attn_W_Q"].T.reshape(D, DH, 4, 2, G).transpose(0, 2, 4, 3, 1).reshape(D, D)
    wk = i["L0_attn_W_K"].T.reshape(D, DH, KV).transpose(0, 2, 1).reshape(D, P)
    wv = i["L0_attn_W_V"].T.reshape(D, DH, KV).transpose(0, 2, 1).reshape(D, P)
    cols = []
    for s in range(SHARED):
        r = slice(s * INTER, (s + 1) * INTER)
        cols += [i["L0_ffn_sw1"][r].T, i["L0_ffn_sw3"][r].T]
        if s == 0:
            cols.append(i["L0_ffn_gate_w"].T)
    for e in range(EXPERTS):
        cols += [i["L0_ffn_W1"][e], i["L0_ffn_W3"][e]]
    w2 = np.concatenate([i["L0_ffn_sw2"].T, i["L0_ffn_W2"].reshape(EXPERTS * INTER, D)], 0)
    order = channel_order()
    win = i["L1_attn_W_in"].reshape(3, D, D)[:, order, :].reshape(3 * D, D).T
    wout = i["L1_attn_W_out"].T[order]
    return np.ascontiguousarray(np.concatenate(
        [fold(np.concatenate([wq, wk, wv], 1)), fold(i["L0_attn_W_O"].T), fold(np.concatenate(cols, 1)), fold(w2),
         fold(win), fold(wout)], 1))


def channel_order():
    return np.concatenate([np.arange(0, D // 2, 2), np.arange(1, D // 2, 2), np.arange(D // 2, D)])


def rope_tables():
    f = np.float32
    pos = np.arange(S, dtype=f).reshape(NT, P)
    inv0 = f(1.0) / f(10000.0) ** (np.arange(0, DH // 2, dtype=f) * f(2.0) / f(DH))
    ang0 = pos[:, :, None] * inv0
    scale = np.concatenate([np.full(HEADS, 1.0 / np.sqrt(D)), np.ones(KV)]).astype(f)
    r0 = np.stack([np.cos(ang0), np.sin(ang0)])[:, :, :, None, :] * scale[:, None]
    rot = D // 2
    inv1 = f(1.0) / f(10000.0) ** (np.arange(0, rot, 2, dtype=f) / f(rot))
    ang1 = pos[:, :, None] * inv1
    r1 = np.stack([np.cos(ang1), np.sin(ang1)])
    return (np.ascontiguousarray(r0.transpose(2, 0, 1, 3, 4).reshape(P, -1).astype(f)),
            np.ascontiguousarray(r1.transpose(2, 0, 1, 3).reshape(P, -1).astype(f)))


def kernel(**inputs):
    import concourse.bacc as _bacc
    from concourse.bass_utils import run_bass_kernel_spmd as _run

    i = {k: np.asarray(v) for k, v in inputs.items()}
    r0, r1 = rope_tables()
    order = channel_order()
    arrays = {
        "x": np.ascontiguousarray(i["L0_attn_x"]),
        "wpack": pack_weights(i),
        "tern1": np.ascontiguousarray(fold(i["L1_ffn_w1"].T)),
        "tern2": np.ascontiguousarray(fold(i["L1_ffn_w2"].T)),
        "tern3": np.ascontiguousarray(fold(i["L1_ffn_w3"].T)),
        "rbias": np.ascontiguousarray(i["L0_ffn_router_bias"]),
        "b_in": np.ascontiguousarray(i["L1_attn_b_in"].reshape(3, D)[:, order].reshape(-1)),
        "b_out": np.ascontiguousarray(i["L1_attn_b_out"]),
        "rope0": r0,
        "rope1": r1,
        "eye": np.eye(P, dtype=np.float32),
    }
    nc = _bacc.Bacc("TRN2", target_bir_lowering=False, num_devices=1)
    args = [nc.dram_tensor(f"in_{n}", a.shape, mybir.dt.from_np(a.dtype), kind="ExternalInput").ap()
            for n, a in arrays.items()]
    out = nc.dram_tensor("out_y", (BATCHES, S, D), F32, kind="ExternalOutput").ap()
    build(nc, *args, out)
    r = _run(nc, [{f"in_{n}": a for n, a in arrays.items()}], core_ids=[0])
    return r.results[0]["out_y"]
```

```python
from contextlib import ExitStack

import numpy as np

import concourse.bass as bass
from concourse import mybir

F32 = mybir.dt.float32
F32R = mybir.dt.float32r
U32 = mybir.dt.uint32
ALU = mybir.AluOpType
ACT = mybir.ActivationFunctionType
AX = mybir.AxisListType

P = 128
D = 256
KD = D // P
BATCHES = 8
S = 256
NT = S // P
HEADS, KV, G, DH = 16, 8, 2, 16
EXPERTS, INTER, SHARED = 8, 176, 2
GROUPS = SHARED + EXPERTS
HID = GROUPS * INTER
CHUNKS = -(-HID // P)
FFN_HID = 704
FGROUPS = FFN_HID // INTER
FCHUNKS = -(-FFN_HID // P)
PAIR = 2 * INTER
W13 = GROUPS * PAIR + EXPERTS
LN_EPS = 1e-5
NORM_EPS2 = 1e-24
QUANT_EPS = 1e-8

O_QKV = 0
O_WO = O_QKV + KD * (D + 2 * P)
O_W13 = O_WO + KD * D
O_W2 = O_W13 + KD * W13
O_WIN = O_W2 + CHUNKS * D
O_WOUT = O_WIN + KD * 3 * D
WCOLS = O_WOUT + KD * D
PIECES = 8
PW = -(-(WCOLS - O_W13) // PIECES)
WCUTS = [0, O_W13] + [min(O_W13 + PW * (n + 1), WCOLS) for n in range(PIECES)]
TW = KD * FFN_HID
STAGE = max(PW, O_W13)
LOADS = (0, 1, 2, 3, 4, "tern3", 5, 6, 7, 8)
PREP = ((1, 0), (2, "ready"), (2, 1), (3, 2), (4, 3), (5, 4), (6, "abs"), (7, "thresholds"),
        (10, "quant 3"), (11, "quant 1"), (12, 5), (15, 6), (17, 7), (23, 8))
SLOTS = 3

T_LAG, W_LAG = 1, 3
FT_LAG, FW_LAG = 0, 2
S_LAG, P_LAG = 2, 3
XCOPY_AT = 4
SCHED = "00101010101010102010200211110111101113011010"

ZSTEP = P
ZHALF = 3 * P + 2 * DH
ZCOLS = 2 * ZHALF + DH


def zwindow(head):
    kv = head // G
    return (kv // 4) * ZHALF + DH + ZSTEP * (kv % 4) - DH * (head % 8)


def head_of(h):
    return ((h // 4) * 2 + h % 2) * G + (h // 2) % G


def group_start(gi):
    return gi * PAIR + (EXPERTS if gi else 0)


def build(nc, x, wpack, tern12, tern3, rbias, b_in, b_out, rope0, rope1, eye, out):
    ctx = ExitStack()
    with ctx:
        def sb(name, cols, dt=F32, where=ctx):
            return where.enter_context(nc.sbuf_tensor(name, [P, cols], dt))

        def sem(name):
            return ctx.enter_context(nc.semaphore(name))

        w_hi = sb("w_hi", WCOLS, F32R)
        w_lo = sb("w_lo", WCOLS, F32R)
        w12q = sb("w12q", 2 * TW, F32R)
        w3q = sb("w3q", FCHUNKS * D, F32R)
        ident = sb("ident", P)
        ones = sb("ones", P)
        cos0 = sb("rope0_sb", 2 * NT * 192)
        cs1 = sb("rope1_sb", 2 * NT * 64)
        bin_sb = sb("bin_sb", 3 * D)
        bout_sb = sb("bout_sb", D)
        rb_sb = sb("rb_sb", EXPERTS)
        mhalf = sb("mhalf", NT)
        epst = sb("epst", NT)
        iot = sb("iot", EXPERTS)
        fence = sb("fence", 2)
        a_st = sb("a_st", NT * 6)
        a_mv = sb("a_mv", NT * 2)
        a_ve = sb("a_ve", NT)
        a_rstd = sb("a_rstd", NT)
        nmax = [sb(f"nmax{i}", NT) for i in range(2)]
        rsum = sb("rsum", NT * HEADS)
        b_st = sb("b_st", NT * 6)
        b_mv = sb("b_mv", NT * 2)
        b_ve = sb("b_ve", NT)
        b_rstd = sb("b_rstd", NT)
        r_e = sb("r_e", EXPERTS)
        r_sc = sb("r_sc", EXPERTS)
        r_sel = sb("r_sel", EXPERTS)
        r_top = sb("r_top", 8)
        r_idx = sb("r_idx", 8, U32)
        r_idf = sb("r_idf", 8)
        r_m = sb("r_m", EXPERTS)
        r_sum = sb("r_sum", 4)
        gate = sb("gate", EXPERTS)
        ssq = sb("ssq", NT)
        ssm = sb("ssm", NT)
        krn = sb("krn", NT)
        asum = sb("asum", 3)
        thr = sb("thr", 3 * 2)

        xA = sb("xA", NT * D)
        qT = sb("qT", 8 * S, F32R)
        kT = sb("kT", 4 * S, F32R)
        z = sb("z", NT * ZCOLS)
        qs = sb("qs", 1024, F32R)
        ks = sb("ks", 512, F32R)
        with ExitStack() as early:
            ahT_hi = sb("ahT_hi", NT * D, F32R, early)
            ahT_lo = sb("ahT_lo", NT * D, F32R, early)
            hA = sb("hA", NT * D, F32, early)
            t1A = sb("t1A", 384, F32, early)
            t2A = sb("t2A", 384, F32, early)
        cT_hi = sb("cT_hi", NT * D, F32R)
        cT_lo = sb("cT_lo", NT * D, F32R)
        pr = [sb(f"pr{i}", NT * S) for i in range(2)]
        pT = [sb(f"pT{i}", NT * S) for i in range(2)]

        with ExitStack() as prep:
            stage = [sb(f"stage{i}", STAGE, F32, prep) for i in range(SLOTS)]
            stage12 = sb("stage12", 2 * TW, F32, prep)
        xM = sb("xM", NT * D)
        xB = sb("xB", NT * D)
        hB = sb("hB", NT * D)
        bhT_hi = sb("bhT_hi", NT * D, F32R)
        bhT_lo = sb("bhT_lo", NT * D, F32R)
        hid = sb("hid", HID)
        th = [sb(f"th{i}", INTER) for i in range(2)]
        up = [sb(f"up{i}", INTER) for i in range(2)]
        with ExitStack() as attn1:
            rt1, rt2, sq = (sb(n, 2 * P, F32, attn1) for n in ("rt1", "rt2", "sq"))
        hdT_hi = [sb(f"hdT_hi{i}", 512, F32R) for i in range(2)]
        hdT_lo = [sb(f"hdT_lo{i}", 512, F32R) for i in range(2)]

        bank = [ctx.enter_context(nc.psum_tensor(f"bank{i}", [P, 512], F32)) for i in range(8)]
        bS, bPT, bC = bank[0:2], bank[2], bank[3]
        bG, bTB, bY = bank[4:6], bank[6], bank[7]
        bHT = [bTB, bG[1]]

        def v2(t, a):
            return t[:, :].rearrange("p (a n) -> p a n", a=a)

        xA_t, xM_t, xB_t, hA_t, hB_t = (v2(t, NT) for t in (xA, xM, xB, hA, hB))
        cosr = cos0[:, :].rearrange("p (f t h j) -> p f t h j", f=2, t=NT, j=8)
        c1r = cs1[:, :].rearrange("p (f t j) -> p f t j", f=2, t=NT)
        x_b = x.rearrange("b (t p) d -> b p t d", p=P)
        out_b = out.rearrange("b (t p) d -> b p t d", p=P)

        def W(part, at, k, width, a, b):
            return part[:, at + k * width + a:at + k * width + b]

        block = ctx.enter_context(nc.Block())

        stage_in = [sem(f"stage_in{i}") for i in range(SLOTS)]
        consts_in, x_in, xB_free = sem("consts_in"), sem("x_in"), sem("xB_free")
        ident_in, rope_in, tern12_in = (sem(f"{n}_in") for n in ("ident", "rope", "tern12"))
        setup_pool, zeros_ready = sem("setup_pool"), sem("zeros_ready")
        split_hi, split_hi_dve, split_lo = sem("split_hi"), sem("split_hi_dve"), sem("split_lo")
        abs_sum, abs_act, abs_total, tern_cut, tern_pool, tern_dve, tern_done, quant_chain = sem("abs_sum"), sem("abs_act"), sem("abs_total"), sem("tern_cut"), sem("tern_pool"), sem("tern_dve"), sem("tern_done"), sem("quant_chain")
        a_chain, a_mv_r, a_ve_r, a_rstd_r, a_h_r = (sem(f"a_{n}") for n in ("chain", "mv_r", "ve_r", "rstd_r", "h_r"))
        a_hps, a_hhi, a_hlo, a_rot = sem("a_hps"), sem("a_hhi"), sem("a_hlo"), sem("a_rot")
        a_qkv, a_raw, a_rope, a_sthi, a_stlo = (sem(f"a_{n}") for n in ("qkv", "raw", "rope", "sthi", "stlo"))
        a_stT, a_stev_act, a_stev_dve = sem("a_stT"), sem("a_stev_act"), sem("a_stev_dve")
        a_score, a_nmax, a_exp, a_rrec, a_rT, a_rcopy, a_ctx = (sem(f"a_{n}") for n in ("score", "nmax", "exp", "rrec", "rT", "rcopy", "ctx"))
        a_pps, a_pT, a_pv = (sem(f"a_{n}") for n in ("pps", "pT", "pv"))
        a_chi, a_clo, a_wo, a_xmid = (sem(f"a_{n}") for n in ("chi", "clo", "wo", "xmid"))
        b_chain, b_xcopy, b_mv_r, b_ve_r, b_rstd_r, b_h_r = (sem(f"b_{n}") for n in ("chain", "xcopy", "mv_r", "ve_r", "rstd_r", "h_r"))
        b_hps, b_hhi, b_hlo = sem("b_hps"), sem("b_hhi"), sem("b_hlo")
        b_grp, b_route, b_gate, b_gated, b_th, b_silu, b_hid = (sem(f"b_{n}") for n in ("grp", "route", "gate", "gated", "th", "silu", "hid"))
        b_tps, b_thi, b_tlo, b_down, b_res1 = (sem(f"b_{n}") for n in ("tps", "thi", "tlo", "down", "res1"))
        b_qkv, b_qkvev, b_pool, b_ropeq, b_rot, b_rope, b_ssq, b_ssm, b_krn, b_kv, b_A, b_y = (
            sem(f"b_{n}") for n in ("qkv", "qkvev", "pool", "ropeq", "rot", "rope", "ssq", "ssm", "krn", "kv", "A", "y"))
        b_attn, b_hb, b_res, b_res2, b_fin = (sem(f"b_{n}") for n in ("attn", "hb", "res", "res2", "fin"))

        def at(b, per, k):
            return b * per + k

        NLN = 3
        NM, NF = NT * GROUPS, NT * FGROUPS
        NG = NM + NF
        TQ, FQ = -(-CHUNKS // 4), -(-FCHUNKS // 4)
        NQ = NT * (TQ + FQ)

        def chunks_of(n_hid, q):
            return [(c, min(P, n_hid - c * P)) for c in range(4 * q, min(4 * q + 4, -(-n_hid // P)))]

        def groups_for(n_hid, q):
            return min(-(-(4 * q + 4) * P // INTER), n_hid // INTER)

        def sets_at(n_hid, slot, lag):
            n, nq = n_hid // INTER, -(-(-(-n_hid // P)) // 4)
            return [(t, q) for t in range(NT) for q in range(nq) if t * n + groups_for(n_hid, q) + lag == slot]

        MLP_SLOTS = NM + W_LAG + 1
        FFN_SLOTS = NF + FW_LAG + 1
        LN1_EARLY = GROUPS + W_LAG + 1
        NT_B = (NLN + 1) * NT

        A_SLOTS = 7 + HEADS + P_LAG + 5
        B_SLOTS = MLP_SLOTS + 9 + FFN_SLOTS
        PREP_SLOTS = len(PREP)
        A_BEHIND = a_schedule(B_SLOTS, A_SLOTS)

        def together(first, second, n_first, n_second, behind):
            done = 0
            for i in range(n_first):
                next(first)
                for _ in range(behind[i]):
                    next(second)
                    done += 1
            assert done == n_second and not list(first) and not list(second), (len(list(first)), len(list(second)))

        def program(eng, prepare, stream_a, stream_b):
            together(stream_a(0), prepare(), A_SLOTS, PREP_SLOTS, [sum(slot == i for slot, _ in PREP) for i in range(A_SLOTS)])
            with eng.Fori(0, BATCHES - 1) as b:
                together(stream_b(b), stream_a(b + 1), B_SLOTS, A_SLOTS, A_BEHIND)
            for _ in stream_b(BATCHES - 1):
                pass

        def stage_of(n):
            return stage[LOADS.index(n) % SLOTS]

        def staged(n):
            load = LOADS.index(n)
            return stage_in[load % SLOTS], 16 * (load // SLOTS + 1)

        def tern_views(j):
            if j == 2:
                return w3q[:, :], stage_of("tern3")[:, 0:FCHUNKS * D]
            return tuple(w[:, :].rearrange("p (g u n) -> p g u n", u=2, n=INTER)[:, :, j, :] for w in (w12q, stage12))

        def hT_bank(k):
            return (bG[1], bTB)[k] if k < NT else bHT[k % NT]

        def set_bank(m):
            return bG[0] if m == NQ - 1 else bTB

        def vview(ps, u):
            a = D + P + u * 4 * DH
            return ps[:, a:a + 4 * DH].rearrange("p (v d) -> p v d", d=DH)

        def zview(z, t, u):
            first, step = 1 + u * (ZHALF // DH), ZSTEP // DH
            return z[:, t * ZCOLS:(t + 1) * ZCOLS].rearrange("p (c d) -> p c d", d=DH)[:, first:first + 3 * step + 1:step, :]

        def stack_dst(j, t):
            dst = qT if j < 2 else kT
            a = 4 * j if j < 2 else 0
            return dst[:, :].rearrange("p (k n) -> p k n", n=S)[:, a:a + 4, t * P:(t + 1) * P]

        q4 = qs[:, :].rearrange("p (h s d) -> p h s d", s=4, d=DH)
        k4 = ks[:, :].rearrange("p (h s d) -> p h s d", s=4, d=DH)
        q1 = t1A[:, 0:D].rearrange("p (h o d) -> p h o d", o=1, d=DH).broadcast_to([P, HEADS, 2, DH])
        k1 = t1A[:, D:D + P].rearrange("p (h o d) -> p h o d", o=1, d=DH).broadcast_to([P, KV, 2, DH])
        raw = hA[:, 0:384]
        qk_all = hid[:, 0:NT * 2 * D].rearrange("p (t u n) -> p t u n", t=NT, u=2)
        kv = hid[:, NT * 2 * D:NT * 3 * D].rearrange("p (t n) -> p t n", t=NT)

        @block.sync
        def _(sp):
            sp.dma_start(xA_t, x_b[0]).then_inc(x_in, 16)
            sp.dma_start(ident[:, :], eye).then_inc(ident_in, 16)
            for i, n in enumerate(LOADS):
                if i >= SLOTS:
                    last = LOADS[i - SLOTS]
                    if last == "tern3":
                        sp.wait_ge(tern_done, 1)
                    else:
                        sp.wait_ge(split_lo, last + 1)
                if n == "tern3":
                    sp.dma_start(stage12[:, :], tern12).then_inc(tern12_in, 16)
                    src = tern3
                else:
                    src = wpack[:, WCUTS[n]:WCUTS[n + 1]]
                sp.dma_start(stage_of(n)[:, 0:src.shape[-1]], src).then_inc(stage_in[i % SLOTS], 16)
                if n == 0:
                    sp.dma_start(cos0[:, :], rope0).then_inc(rope_in, 16)
            sp.dma_start(cs1[:, :], rope1).then_inc(consts_in, 16)
            for t, src, n in ((bin_sb, b_in, 3 * D), (bout_sb, b_out, D), (rb_sb, rbias, EXPERTS)):
                sp.dma_start(t[:, :], src.rearrange("(a n) -> a n", a=1).broadcast_to([P, n])).then_inc(consts_in, 16)

            def load_x(b):
                sp.wait_ge(a_xmid, at(b - 1, NT, NT))
                sp.dma_start(xA_t, x_b[b]).then_inc(x_in, 16)

            def store(b):
                sp.wait_ge(b_fin, at(b, NT, NT))
                sp.dma_start(out_b[b], xB_t).then_inc(xB_free, 16)

            with sp.Fori(1, BATCHES) as b:
                load_x(b)
                store(b - 1)
            store(BATCHES - 1)
            sp.wait_ge(xB_free, 16 * (BATCHES + 1))

        @block.gpsimd
        def _(pool):
            nc.gpsimd.memset(ones[:, :], 1.0).then_inc(setup_pool, 1)
            nc.gpsimd.memset(fence[:, 1:2], 0.0).then_inc(xB_free, 16)
            nc.gpsimd.memset(mhalf[:, :], -0.5).then_inc(setup_pool, 1)
            nc.gpsimd.memset(epst[:, :], LN_EPS).then_inc(setup_pool, 1)
            nc.gpsimd.iota(iot[:, :], pattern=[[1, EXPERTS]], base=0, channel_multiplier=0,
                           allow_small_or_imprecise_dtypes=True).then_inc(setup_pool, 1)
            pool.wait_ge(setup_pool, 4)

            def prepare():
                for _, step in PREP:
                    if step == "quant 3":
                        pool.wait_ge(quant_chain, 3)
                        w, raw_w = tern_views(1)
                        nc.gpsimd.tensor_scalar(w, raw_w, thr[:, 4:5], None, ALU.is_lt)
                        nc.gpsimd.tensor_scalar(raw_w, raw_w, thr[:, 1:2], None, ALU.is_gt).then_inc(tern_cut, 1)
                        pool.wait_ge(tern_cut, 1)
                        nc.gpsimd.tensor_tensor(w, raw_w, w.bitcast(F32), ALU.subtract).then_inc(tern_pool, 1)
                    if step == PIECES:
                        pool.wait_ge(rope_in, 16)
                        pool.wait_ge(tern_pool, 1)
                        pool.wait_ge(consts_in, 16 * 4)
                    yield

            def rstd(mv, ve, rs, s_mv, s_ve, s_rs, n_mv, n, t0=0, t1=NT):
                pool.wait_ge(s_mv, n_mv)
                nc.gpsimd.tensor_tensor(ve[:, t0:t1], v2(mv, NT)[:, t0:t1, 1], epst[:, t0:t1], ALU.add).then_inc(s_ve, 1)
                pool.wait_ge(s_ve, n)
                nc.gpsimd.tensor_tensor(rs[:, t0:t1], ve[:, t0:t1], mhalf[:, t0:t1], ALU.pow).then_inc(s_rs, 1)

            def rotate(src, t1, t2, out0, cos, sin, s, at_):
                nc.gpsimd.tensor_tensor(t1, src, cos, ALU.mult)
                nc.gpsimd.tensor_tensor(t2[:, :, 0, :], src[:, :, 1, :], sin, ALU.mult)
                nc.gpsimd.tensor_tensor(t2[:, :, 1, :], src[:, :, 0, :], sin, ALU.mult).then_inc(s, 1)
                pool.wait_ge(s, at_)
                nc.gpsimd.tensor_tensor(out0[:, :, 0, :], t1[:, :, 0, :], t2[:, :, 0, :], ALU.subtract)
                return nc.gpsimd.tensor_tensor(out0[:, :, 1, :], t1[:, :, 1, :], t2[:, :, 1, :], ALU.add)

            def rope_a(b, t):
                pool.wait_ge(a_raw, at(b, NT, t + 1))
                t1 = t1A[:, :].rearrange("p (h e j) -> p h e j", e=2, j=8)
                t2 = t2A[:, :].rearrange("p (h e j) -> p h e j", e=2, j=8)
                cosb = cosr[:, 0, t].rearrange("p h (o j) -> p h o j", o=1).broadcast_to([P, 24, 2, 8])
                rotate(raw.rearrange("p (h e j) -> p h e j", e=2, j=8), t1, t2, t1, cosb, cosr[:, 1, t],
                       a_rot, at(b, NT, t + 1)).then_inc(a_rope, 1)

            def stack_lo(b, t):
                pool.wait_ge(a_sthi, at(b, NT, t + 1))
                nc.gpsimd.tensor_tensor(q4[:, :, 2:4, :], q1, q4[:, :, 0:2, :].bitcast(F32), ALU.subtract)
                nc.gpsimd.tensor_tensor(k4[:, :, 1:4:2, :], k1, k4[:, :, 0:4:2, :].bitcast(F32), ALU.subtract).then_inc(a_stlo, 1)

            def stream_a(b):
                rstd(a_mv, a_ve, a_rstd, a_mv_r, a_ve_r, a_rstd_r, at(b, NT, NT), at(b, 1, 1))
                yield
                yield
                yield
                if not isinstance(b, int):
                    rope_a(b, 0)
                yield
                if not isinstance(b, int):
                    stack_lo(b, 0)
                    pool.wait_ge(a_stlo, at(b, NT, 1))
                    rope_a(b, 1)
                yield
                if not isinstance(b, int):
                    stack_lo(b, 1)
                yield
                yield
                for _ in range(HEADS + P_LAG + 2):
                    yield
                for t in range(NT):
                    norm_b(b, 0, t)
                for _ in range(3):
                    yield

            def norm_b(b, n, t):
                k = at(b, NLN * NT, n * NT + t + 1)
                rstd(b_mv, b_ve, b_rstd, b_mv_r, b_ve_r, b_rstd_r, k, k, t, t + 1)

            def rope_b(b, t):
                pool.wait_ge(b_qkvev, at(b, NT, t + 1))
                if t > 0:
                    pool.wait_ge(b_ropeq, at(b, NT, t))
                t1 = rt1[:, 0:P].rearrange("p (u e j) -> p u e j", u=1, e=2)
                t2 = rt2[:, 0:P].rearrange("p (u e j) -> p u e j", u=1, e=2)
                rot = qk_all[:, t, 0:1, 0:P].rearrange("p u (e j) -> p u e j", e=2)
                cb = c1r[:, 0, t].rearrange("p (o w j) -> p o w j", o=1, w=1).broadcast_to([P, 1, 2, 64])
                sn = c1r[:, 1, t].rearrange("p (o j) -> p o j", o=1)
                rotate(rot, t1, t2, rot, cb, sn, b_pool, at(b, NT, t + 1)).then_inc(b_ropeq, 1)

            def key_norm(b, t):
                pool.wait_ge(b_ssm, at(b, NT, t + 1))
                nc.gpsimd.tensor_tensor(krn[:, t:t + 1], ssm[:, t:t + 1], mhalf[:, 0:1], ALU.pow).then_inc(b_krn, 1)

            def stream_b(b):
                for s in range(MLP_SLOTS):
                    if s < NM:
                        gi = s % GROUPS
                        pool.wait_ge(b_silu, at(b, NM, s + 1))
                        if gi == SHARED:
                            pool.wait_ge(b_gate, at(b, NT, s // GROUPS + 1))
                            nc.gpsimd.tensor_tensor(up[s % 2][:, :], up[s % 2][:, :], gate[:, 0:1].broadcast_to([P, INTER]),
                                                    ALU.mult).then_inc(b_gated, 1)
                            pool.wait_ge(b_gated, at(b, NT, s // GROUPS + 1))
                        nc.gpsimd.tensor_tensor(hid[:, gi * INTER:(gi + 1) * INTER], th[s % 2][:, :], up[s % 2][:, :],
                                                ALU.mult).then_inc(b_hid, 1)
                    if s == LN1_EARLY:
                        norm_b(b, 1, 0)
                    if s == MLP_SLOTS - 1:
                        norm_b(b, 1, 1)
                    yield
                rope_b(b, 0)
                yield
                key_norm(b, 0)
                pool.wait_ge(b_hps, at(b, NT_B, 4))
                nc.gpsimd.tensor_tensor(hB_t, hB_t, bout_sb[:, :].rearrange("p (o n) -> p o n", o=1).broadcast_to([P, NT, D]),
                                        ALU.add).then_inc(b_hb, 1)
                yield
                key_norm(b, 1)
                rope_b(b, 1)
                yield
                pool.wait_ge(b_hb, at(b, 1, 1))
                nc.gpsimd.tensor_tensor(xB[:, :], xB[:, :], hB[:, :], ALU.add).then_inc(b_res, 1)
                yield
                yield
                yield
                for t in range(NT):
                    norm_b(b, 2, t)
                yield
                yield
                yield
                for s in range(FFN_SLOTS):
                    yield

            program(pool, prepare, stream_a, stream_b)

        @block.scalar
        def _(act):
            def prepare():
                for _, n in PREP:
                    if n == "abs":
                        act.wait_ge(tern12_in, 16)
                        for j in range(2):
                            w, raw_w = tern_views(j)
                            ins = nc.scalar.activation(w, raw_w, ACT.Abs, accum_out=asum[:, j:j + 1])
                        ins.then_inc(abs_act, 1)
                    if isinstance(n, int) and n % 2 == 0:
                        a, b = WCUTS[n], WCUTS[n + 1]
                        act.wait_ge(*staged(n))
                        nc.scalar.activation(w_hi[:, a:b], stage_of(n)[:, 0:b - a], ACT.Copy).then_inc(split_hi, 1)
                    yield

            def take(ps, dst, s_ps, n_ps, s_hi):
                act.wait_ge(s_ps, n_ps)
                nc.scalar.activation(dst, ps, ACT.Copy).then_inc(s_hi, 1)

            def project_a(b, t):
                act.wait_ge(a_qkv, at(b, NT, t + 1))
                for u in range(2):
                    nc.scalar.activation(zview(z, t, u), vview(bS[t], u), ACT.Copy)
                nc.scalar.activation(raw, bS[t][:, 0:384], ACT.Copy).then_inc(a_raw, 1)

            def stack_hi(b, t):
                act.wait_ge(a_rope, at(b, NT, t + 1))
                nc.scalar.activation(q4[:, :, 0:2, :], q1, ACT.Copy)
                nc.scalar.activation(k4[:, :, 0:4:2, :], k1, ACT.Copy).then_inc(a_sthi, 1)

            def stack_copy(b, t):
                for j in range(3):
                    n = 3 * t + j
                    if n % 2 == 0:
                        act.wait_ge(a_stT, at(b, 3 * NT, n + 1))
                        nc.scalar.activation(stack_dst(j, t), v2(bPT, 4), ACT.Copy).then_inc(a_stev_act, 1)

            def stream_a(b):
                yield
                yield
                take(bPT[:, :], ahT_hi[:, :], a_hps, at(b, 1, 1), a_hhi)
                yield
                project_a(b, 0)
                yield
                stack_hi(b, 0)
                project_a(b, 1)
                yield
                stack_copy(b, 0)
                stack_hi(b, 1)
                yield
                stack_copy(b, 1)
                yield
                for i in range(HEADS + P_LAG):
                    if S_LAG <= i < HEADS + S_LAG:
                        h = i - S_LAG
                        if h >= 2:
                            act.wait_ge(a_pv, at(b, HEADS, h - 1))
                        take(bPT[:, :], pT[h % 2][:, :], a_pps, at(b, HEADS, h + 1), a_pT)
                    if i < HEADS:
                        h = i
                        act.wait_ge(a_nmax, at(b, HEADS, h + 1))
                        for st in range(NT):
                            ins = nc.scalar.activation(pr[h % 2][:, st * S:(st + 1) * S], bS[h % 2][:, st * S:(st + 1) * S], ACT.Exp,
                                                       bias=nmax[h % 2][:, st:st + 1], accum_out=rsum[:, st * HEADS + head_of(h):st * HEADS + head_of(h) + 1])
                        ins.then_inc(a_exp, 1)
                    yield
                take(bPT[:, :], pr[1][:, :], a_rT, at(b, 1, 1), a_rcopy)
                yield
                take(pr[0][:, :], cT_hi[:, :], a_ctx, at(b, 1, 1), a_chi)
                yield
                yield
                yield
                hT_b(b, 0)
                hT_b(b, 1)
                yield

            def down(b, m, cols):
                if m >= 2:
                    act.wait_ge(b_down, at(b, NQ, m - 1))
                take(set_bank(m)[:, 0:cols], hdT_hi[m % 2][:, 0:cols], b_tps, at(b, NQ, m + 1), b_thi)

            def hT_b(b, k):
                t = k % NT
                take(hT_bank(k)[:, 0:D], bhT_hi[:, t * D:(t + 1) * D], b_hps, at(b, NT_B, k + 1), b_hhi)

            def stream_b(b):
                for s in range(MLP_SLOTS):
                    if s < NM:
                        gi = s % GROUPS
                        g = bG[s % 2]
                        act.wait_ge(b_grp, at(b, NG, s + 1))
                        if gi == 0:
                            nc.scalar.activation(r_e[:, :], g[:, PAIR:PAIR + EXPERTS], ACT.Exp, scale=-1.0).then_inc(b_route, 1)
                        if s >= 2:
                            act.wait_ge(b_hid, at(b, NG, s - 1))
                        nc.scalar.activation(th[s % 2][:, :], g[:, 0:INTER], ACT.Tanh, scale=0.5)
                        if gi == SHARED + 1:
                            act.wait_ge(b_gate, at(b, NT, s // GROUPS + 1))
                        half = 0.5 if gi < SHARED else 1.0 if gi == SHARED else gate[:, gi - SHARED:gi - SHARED + 1]
                        nc.scalar.activation(up[s % 2][:, :], g[:, INTER:PAIR], ACT.Copy, scale=half).then_inc(b_th, 1)
                    for t, q in sets_at(HID, s, T_LAG):
                        down(b, t * TQ + q, P * len(chunks_of(HID, q)))
                    if s == XCOPY_AT:
                        act.wait_ge(a_xmid, at(b, NT, NT))
                        act.wait_ge(xB_free, at(b, 16, 16))
                        nc.scalar.activation(xB[:, :], xM[:, :], ACT.Copy).then_inc(b_xcopy, 1)
                    if s == LN1_EARLY + 2:
                        hT_b(b, 2)
                    yield
                yield
                hT_b(b, 3)
                yield
                for _ in range(3):
                    yield
                hT_b(b, 4)
                hT_b(b, 5)
                yield
                yield
                yield
                hT_b(b, 6)
                hT_b(b, 7)
                yield
                for s in range(FFN_SLOTS):
                    if s < NF:
                        act.wait_ge(b_grp, at(b, NG, NM + s + 1))
                        nc.scalar.activation(th[s % 2][:, :], bG[s % 2][:, 0:INTER], ACT.Tanh, scale=0.5).then_inc(b_th, 1)
                    for t, q in sets_at(FFN_HID, s, FT_LAG):
                        down(b, NT * TQ + t * FQ + q, P * len(chunks_of(FFN_HID, q)))
                    yield

            program(act, prepare, stream_a, stream_b)

        @block.vector
        def _(dve):
            A_LINKS = 2 * NT
            B_LINKS = (NLN - 1) * NT + NT * 11
            links = {"a": 0, "b": 0}
            chain = {"a": a_chain, "b": b_chain}

            def link(s, b, per, ins):
                links[s] += 1
                ins.then_inc(chain[s], 1)
                dve.wait_ge(chain[s], at(b, per, links[s]))

            def hold():
                nc.vector.memset(fence[:, 0:1], 0.0)

            def lnk(b, ins):
                link("b", b, B_LINKS, ins)

            def prepare():
                for _, n in PREP:
                    if isinstance(n, int):
                        a, b = WCUTS[n], WCUTS[n + 1]
                        src = stage_of(n)[:, 0:b - a]
                        if n % 2 == 0:
                            dve.wait_ge(split_hi, n // 2 + 1)
                        else:
                            dve.wait_ge(*staged(n))
                            nc.vector.tensor_copy(w_hi[:, a:b], src).then_inc(split_hi_dve, 1)
                            dve.wait_ge(split_hi_dve, n // 2 + 1)
                        nc.vector.tensor_tensor(w_lo[:, a:b], src, w_hi[:, a:b].bitcast(F32), ALU.subtract).then_inc(split_lo, 1)
                    elif n == "abs":
                        dve.wait_ge(*staged("tern3"))
                        nc.vector.tensor_reduce(asum[:, 2:3], tern_views(2)[1], AX.X, ALU.add,
                                                apply_absolute_value=True).then_inc(abs_sum, 1)
                    elif n == "thresholds":
                        dve.wait_ge(abs_total, 1)
                        nc.vector.tensor_scalar(thr[:, 0:3], bY[:, 0:3], 1.0 / (FFN_HID * D), QUANT_EPS, ALU.mult,
                                                ALU.add).then_inc(quant_chain, 1)
                        dve.wait_ge(quant_chain, 1)
                        nc.vector.tensor_scalar(thr[:, 3:6], thr[:, 0:3], -0.5, None, ALU.mult).then_inc(quant_chain, 1)
                        dve.wait_ge(quant_chain, 2)
                        nc.vector.tensor_scalar(thr[:, 0:3], thr[:, 0:3], 0.5, None, ALU.mult).then_inc(quant_chain, 1)
                    elif n in ("quant 3", "quant 1"):
                        j, done = (2, 0) if n == "quant 3" else (0, 1)
                        dve.wait_ge(quant_chain, 3)
                        w, raw_w = tern_views(j)
                        nc.vector.tensor_scalar(w, raw_w, thr[:, 3 + j:4 + j], None, ALU.is_lt).then_inc(tern_dve, 1)
                        dve.wait_ge(tern_dve, done + 1)
                        nc.vector.scalar_tensor_tensor(out=w, in0=raw_w, scalar=thr[:, j:j + 1], in1=w.bitcast(F32), op0=ALU.is_gt,
                                                       op1=ALU.subtract).then_inc(tern_done, 1)
                    yield

            def stats(s, b, per, xt, st, mv, s_mv, tiles):
                for t in tiles:
                    links[s] += 1
                    nc.vector.bn_stats(st[:, 6 * t:6 * t + 6], xt[:, t, :]).then_inc(chain[s], 1)
                dve.wait_ge(chain[s], at(b, per, links[s]))
                hold()
                for t in tiles:
                    nc.vector.bn_aggr(mv[:, 2 * t:2 * t + 2], st[:, 6 * t:6 * t + 6]).then_inc(s_mv, 1)

            def normalise(xt, ht, mv, rs, s_rs, n, s_h, t):
                dve.wait_ge(s_rs, n)
                nc.vector.tensor_scalar(ht[:, t, :], xt[:, t, :], mv[:, 2 * t:2 * t + 1], rs[:, t:t + 1],
                                        ALU.subtract, ALU.mult).then_inc(s_h, 1)

            def split_l(ps, hi, dst, s_hi, n_hi, s_lo):
                dve.wait_ge(s_hi, n_hi)
                nc.vector.tensor_tensor(dst, ps, hi.bitcast(F32), ALU.subtract).then_inc(s_lo, 1)

            def stack_copy(b, t):
                for j in range(3):
                    n = 3 * t + j
                    if n % 2 == 1:
                        dve.wait_ge(a_stT, at(b, 3 * NT, n + 1))
                        nc.vector.tensor_copy(stack_dst(j, t), v2(bC, 4)).then_inc(a_stev_dve, 1)

            def rope_first(t):
                dve.wait_ge(a_raw, t + 1)
                x, t1, t2 = (u.rearrange("p (h e j) -> p h e j", e=2, j=8) for u in (raw, t1A[:, :], t2A[:, :]))
                cos = cosr[:, 0, t].rearrange("p h (o j) -> p h o j", o=1).broadcast_to([P, 24, 2, 8])
                nc.vector.tensor_tensor(t1, x, cos, ALU.mult)
                nc.vector.tensor_tensor(t2[:, :, 0, :], x[:, :, 1, :], cosr[:, 1, t], ALU.mult)
                nc.vector.tensor_tensor(t2[:, :, 1, :], x[:, :, 0, :], cosr[:, 1, t], ALU.mult).then_inc(a_rot, 1)
                dve.wait_ge(a_rot, t + 1)
                nc.vector.tensor_tensor(t1[:, :, 0, :], t1[:, :, 0, :], t2[:, :, 0, :], ALU.subtract)
                nc.vector.tensor_tensor(t1[:, :, 1, :], t1[:, :, 1, :], t2[:, :, 1, :], ALU.add).then_inc(a_rope, 1)

            def stack_lo_first(t):
                dve.wait_ge(a_sthi, t + 1)
                nc.vector.tensor_tensor(q4[:, :, 2:4, :], q1, q4[:, :, 0:2, :].bitcast(F32), ALU.subtract)
                nc.vector.tensor_tensor(k4[:, :, 1:4:2, :], k1, k4[:, :, 0:4:2, :].bitcast(F32), ALU.subtract).then_inc(a_stlo, 1)

            def stream_a(b):
                links["a"] = 0
                dve.wait_ge(x_in, at(b, 16, 16))
                stats("a", b, A_LINKS, xA_t, a_st, a_mv, a_mv_r, range(NT))
                yield
                for t in range(NT):
                    normalise(xA_t, hA_t, a_mv, a_rstd, a_rstd_r, at(b, 1, 1), a_h_r, t)
                yield
                split_l(bPT[:, :], ahT_hi[:, :], ahT_lo[:, :], a_hhi, at(b, 1, 1), a_hlo)
                yield
                if isinstance(b, int):
                    dve.wait_ge(rope_in, 16)
                    rope_first(0)
                yield
                if isinstance(b, int):
                    stack_lo_first(0)
                    dve.wait_ge(a_stlo, 1)
                    rope_first(1)
                yield
                if isinstance(b, int):
                    stack_lo_first(1)
                stack_copy(b, 0)
                yield
                stack_copy(b, 1)
                yield
                for i in range(HEADS + P_LAG):
                    if i < HEADS:
                        dve.wait_ge(a_score, at(b, HEADS, i + 1))
                        nc.vector.tensor_reduce(nmax[i % 2][:, :], v2(bS[i % 2], NT), AX.X, ALU.max, negate=True).then_inc(a_nmax, 1)
                    if i == HEADS:
                        dve.wait_ge(a_exp, at(b, HEADS, HEADS))
                        nc.vector.reciprocal(rsum[:, :], rsum[:, :]).then_inc(a_rrec, 1)
                        dve.wait_ge(a_pT, at(b, HEADS, HEADS - 1))
                        dve.wait_ge(a_rrec, at(b, 2, 1))
                        nc.vector.tensor_copy(pr[0][:, :].rearrange("p (h d) -> p h d", d=DH),
                                              rsum[:, :].rearrange("p (h o) -> p h o", o=1).broadcast_to([P, NT * HEADS, DH])).then_inc(a_rrec, 1)
                    yield
                dve.wait_ge(a_rcopy, at(b, 1, 1))
                dve.wait_ge(a_pv, at(b, HEADS, HEADS))
                nc.vector.tensor_tensor(pr[0][:, :], bC[:, :], pr[1][:, :], ALU.mult).then_inc(a_ctx, 1)
                yield
                split_l(pr[0][:, :], cT_hi[:, :], cT_lo[:, :], a_chi, at(b, 1, 1), a_clo)
                yield
                for t in range(NT):
                    dve.wait_ge(a_wo, at(b, NT, t + 1))
                    nc.vector.tensor_tensor(xM_t[:, t, :], bS[t][:, 0:D], xA_t[:, t, :], ALU.add).then_inc(a_xmid, 1)
                dve.wait_ge(a_xmid, at(b, NT, NT))
                stats("a", b, A_LINKS, xM_t, b_st, b_mv, b_mv_r, range(NT))
                yield
                for t in range(NT):
                    norm_b(b, 0, t, xM_t)
                yield
                hT_b(b, 0)
                hT_b(b, 1)
                yield

            def route(b, t):
                dve.wait_ge(b_route, at(b, NT, t + 1))
                lnk(b, nc.vector.tensor_scalar(r_sc[:, :], r_e[:, :], 1.0, None, ALU.add))
                lnk(b, nc.vector.reciprocal(r_sc[:, :], r_sc[:, :]))
                lnk(b, nc.vector.tensor_tensor(r_sel[:, :], r_sc[:, :], rb_sb[:, :], ALU.add))
                hold()
                lnk(b, nc.vector.max(r_top[:, :], r_sel[:, :]))
                hold()
                lnk(b, nc.vector.max_index(r_idx[:, :], r_top[:, :], r_sel[:, :]))

            def gates(b):
                lnk(b, nc.vector.tensor_copy(r_idf[:, :], r_idx[:, :]))
                lnk(b, nc.vector.tensor_scalar(r_m[:, :], iot[:, :], r_idf[:, 0:1], None, ALU.is_equal))
                lnk(b, nc.vector.scalar_tensor_tensor(out=r_m[:, :], in0=iot[:, :], scalar=r_idf[:, 1:2], in1=r_m[:, :],
                                                      op0=ALU.is_equal, op1=ALU.add))
                lnk(b, nc.vector.tensor_tensor_reduce(r_m[:, :], r_m[:, :], r_sc[:, :], 1.0, 0.0, ALU.mult, ALU.add, r_sum[:, 0:1]))
                lnk(b, nc.vector.tensor_scalar(r_sum[:, 1:2], r_sum[:, 0:1], 1e-12, None, ALU.max))
                lnk(b, nc.vector.reciprocal(r_sum[:, 2:3], r_sum[:, 1:2]))
                nc.vector.tensor_scalar(gate[:, :], r_m[:, :], r_sum[:, 2:3], 0.5, ALU.mult, ALU.mult).then_inc(b_gate, 1)

            def down(b, m, cols):
                split_l(set_bank(m)[:, 0:cols], hdT_hi[m % 2][:, 0:cols], hdT_lo[m % 2][:, 0:cols], b_thi, at(b, NQ, m + 1), b_tlo)

            def stats_b(b, tiles):
                stats("b", b, B_LINKS, xB_t, b_st, b_mv, b_mv_r, tiles)

            def norm_b(b, n, t, x=xB_t):
                normalise(x, hB_t, b_mv, b_rstd, b_rstd_r, at(b, NLN * NT, n * NT + t + 1), b_h_r, t)

            def hT_b(b, k):
                t = k % NT
                split_l(hT_bank(k)[:, 0:D], bhT_hi[:, t * D:(t + 1) * D], bhT_lo[:, t * D:(t + 1) * D], b_hhi, at(b, NT_B, k + 1), b_hlo)

            def bias_qkv(b, t):
                dve.wait_ge(b_qkv, at(b, NT, t + 1))
                nc.vector.tensor_tensor(kv[:, t], bG[1][:, 0:D], bin_sb[:, 2 * D:3 * D], ALU.add)
                nc.vector.tensor_tensor(qk_all[:, t], v2(bG[0], 2), bin_sb[:, 0:2 * D].rearrange("p (u n) -> p u n", u=2),
                                        ALU.add).then_inc(b_qkvev, 1)

            def key_rope(b, t):
                dve.wait_ge(b_qkvev, at(b, NT, t + 1))
                k = qk_all[:, t, 1, 0:P].rearrange("p (e j) -> p e j", e=2)
                t1, t2 = (r[:, P:2 * P].rearrange("p (e j) -> p e j", e=2) for r in (rt1, rt2))
                cos = c1r[:, 0, t].rearrange("p (o j) -> p o j", o=1).broadcast_to([P, 2, 64])
                sin = c1r[:, 1, t]
                nc.vector.tensor_tensor(t1, k, cos, ALU.mult)
                nc.vector.tensor_tensor(t2[:, 0, :], k[:, 1, :], sin, ALU.mult)
                nc.vector.tensor_tensor(t2[:, 1, :], k[:, 0, :], sin, ALU.mult).then_inc(b_rot, 1)
                dve.wait_ge(b_rot, at(b, NT, t + 1))
                nc.vector.tensor_tensor(k[:, 0, :], t1[:, 0, :], t2[:, 0, :], ALU.subtract)
                nc.vector.tensor_tensor(k[:, 1, :], t1[:, 1, :], t2[:, 1, :], ALU.add).then_inc(b_rope, 1)

            def key_square(b, t):
                key_rope(b, t)
                dve.wait_ge(b_rope, at(b, NT, t + 1))
                nc.vector.tensor_tensor_reduce(sq[:, :], qk_all[:, t, 1, :], qk_all[:, t, 1, :], 1.0, 0.0, ALU.mult, ALU.add,
                                               ssq[:, t:t + 1]).then_inc(b_ssq, 1)
                dve.wait_ge(b_ssq, at(b, NT, t + 1))
                nc.vector.tensor_scalar(ssm[:, t:t + 1], ssq[:, t:t + 1], NORM_EPS2, None, ALU.max).then_inc(b_ssm, 1)

            def key_value(b, t):
                dve.wait_ge(b_krn, at(b, NT, t + 1))
                nc.vector.scalar_tensor_tensor(out=kv[:, t], in0=qk_all[:, t, 1, :], scalar=krn[:, t:t + 1], in1=kv[:, t],
                                               op0=ALU.mult, op1=ALU.mult).then_inc(b_kv, 1)

            def stream_b(b):
                links["b"] = 0
                for s in range(MLP_SLOTS):
                    if s == MLP_SLOTS - 1:
                        bias_qkv(b, 0)
                    if s < NM:
                        dve.wait_ge(b_th, at(b, NG, s + 1))
                        u = th[s % 2][:, :]
                        nc.vector.scalar_tensor_tensor(out=u, in0=u, scalar=1.0, in1=bG[s % 2][:, 0:INTER], op0=ALU.add,
                                                       op1=ALU.mult).then_inc(b_silu, 1)
                        if s % GROUPS == 1:
                            route(b, s // GROUPS)
                        if s % GROUPS == 2:
                            gates(b)
                    for t, q in sets_at(HID, s, W_LAG):
                        if q == TQ - 1:
                            dve.wait_ge(b_down, at(b, NQ, (t + 1) * TQ))
                            dve.wait_ge(b_xcopy, at(b, 1, 1))
                            nc.vector.tensor_tensor(xB_t[:, t, :], bY[:, 0:D], xB_t[:, t, :], ALU.add).then_inc(b_res1, 1)
                    for t, q in sets_at(HID, s, T_LAG):
                        down(b, t * TQ + q, P * len(chunks_of(HID, q)))
                    if s == LN1_EARLY:
                        dve.wait_ge(b_res1, at(b, NT, 1))
                        stats_b(b, [0])
                    if s == LN1_EARLY + 1:
                        norm_b(b, 1, 0)
                    if s == LN1_EARLY + 2:
                        hT_b(b, 2)
                    if s == MLP_SLOTS - 1:
                        dve.wait_ge(b_res1, at(b, NT, NT))
                        stats_b(b, [1])
                    yield
                norm_b(b, 1, 1)
                yield
                hT_b(b, 3)
                key_square(b, 0)
                yield
                bias_qkv(b, 1)
                key_value(b, 0)
                key_square(b, 1)
                yield
                key_value(b, 1)
                yield
                yield
                dve.wait_ge(b_A, at(b, 1, 1))
                for t in range(NT):
                    dve.wait_ge(b_ropeq, at(b, NT, t + 1))
                    nc.vector.tensor_tensor(qk_all[:, t, 0, :], bY[:, 0:D], qk_all[:, t, 0, :], ALU.mult).then_inc(b_y, 1)
                hT_b(b, 4)
                hT_b(b, 5)
                yield
                for t in range(NT):
                    dve.wait_ge(b_attn, at(b, NT, t + 1))
                    if t == 0:
                        dve.wait_ge(b_res, at(b, 1, 1))
                    nc.vector.tensor_tensor(xB_t[:, t, :], (bY, bG[0])[t][:, 0:D], xB_t[:, t, :], ALU.add).then_inc(b_res2, 1)
                    dve.wait_ge(b_res2, at(b, NT, t + 1))
                    stats_b(b, [t])
                yield
                for t in range(NT):
                    norm_b(b, 2, t)
                yield
                hT_b(b, 6)
                hT_b(b, 7)
                yield
                for s in range(FFN_SLOTS):
                    if s < NF:
                        dve.wait_ge(b_th, at(b, NG, NM + s + 1))
                        nc.vector.scalar_tensor_tensor(out=hid[:, s * INTER:(s + 1) * INTER], in0=th[s % 2][:, :], scalar=1.0,
                                                       in1=bG[s % 2][:, INTER:PAIR], op0=ALU.add, op1=ALU.mult).then_inc(b_hid, 1)
                    for t, q in sets_at(FFN_HID, s, FW_LAG):
                        if q == FQ - 1:
                            dve.wait_ge(b_down, at(b, NQ, NT * TQ + (t + 1) * FQ))
                            nc.vector.scalar_tensor_tensor(out=xB_t[:, t, :], in0=bY[:, 0:D], scalar=0.5, in1=xB_t[:, t, :],
                                                           op0=ALU.mult, op1=ALU.add).then_inc(b_fin, 1)
                    for t, q in sets_at(FFN_HID, s, FT_LAG):
                        down(b, NT * TQ + t * FQ + q, P * len(chunks_of(FFN_HID, q)))
                    yield

            nc.vector.memset(z[:, :], 0.0).then_inc(zeros_ready, 1)
            dve.wait_ge(zeros_ready, 1)
            program(dve, prepare, stream_a, stream_b)
            assert links["a"] == A_LINKS and links["b"] == B_LINKS, links

        @block.tensor
        def _(pe):
            def prepare():
                for _, step in PREP:
                    if step == "ready":
                        pe.wait_ge(split_lo, 1)
                    if step == "thresholds":
                        pe.wait_ge(setup_pool, 4)
                        pe.wait_ge(abs_sum, 1)
                        pe.wait_ge(abs_act, 1)
                        nc.tensor.matmul(bY[:, 0:3], ones[:, :], asum[:, :], start=True, stop=True).then_inc(abs_total, 1)
                    yield

            def exact(ps, hi, lo, at_, width, a, b_, kn):
                for k in range(kn):
                    nc.tensor.matmul(ps, hi(k), W(w_hi, at_, k, width, a, b_), start=k == 0, stop=False)
                    nc.tensor.matmul(ps, hi(k), W(w_lo, at_, k, width, a, b_), start=False, stop=False)
                    ins = nc.tensor.matmul(ps, lo(k), W(w_hi, at_, k, width, a, b_), start=False, stop=k == kn - 1)
                return ins

            def tr(dst, src, s_done, last):
                ins = nc.tensor.transpose(dst, src, ident[:, :])
                if last:
                    ins.then_inc(s_done, 1)

            def hT(buf, t):
                return lambda k: buf[:, (t * KD + k) * P:(t * KD + k + 1) * P]

            def stacks(b, t):
                pe.wait_ge(a_stlo, at(b, NT, t + 1))
                for j in range(3):
                    n = 3 * t + j
                    dst = (bPT, bC)[n % 2]
                    if n >= 2:
                        pe.wait_ge((a_stev_act, a_stev_dve)[n % 2], at(b, 3, n // 2))
                    for i in range(4):
                        src = qs if j < 2 else ks
                        c = (4 * j if j < 2 else 0) + i
                        tr(dst[:, i * P:(i + 1) * P], src[:, c * P:(c + 1) * P].bitcast(F32), a_stT, i == 3)

            def stream_a(b):
                yield
                yield
                for t in range(NT):
                    pe.wait_ge(a_h_r, at(b, NT, t + 1))
                    for k in range(KD):
                        tr(bPT[:, (t * KD + k) * P:(t * KD + k + 1) * P], hA_t[:, t, k * P:(k + 1) * P], a_hps, t == NT - 1 and k == KD - 1)
                yield
                pe.wait_ge(a_hlo, at(b, 1, 1))
                for t in range(NT):
                    exact(bS[t][:, :], hT(ahT_hi, t), hT(ahT_lo, t), O_QKV, D + 2 * P, 0, D + 2 * P, KD).then_inc(a_qkv, 1)
                    yield
                for t in range(NT):
                    stacks(b, t)
                    yield
                pe.wait_ge(a_stev_act, at(b, 3, 3))
                pe.wait_ge(a_stev_dve, at(b, 3, 3))
                pe.wait_ge(a_raw, at(b, NT, NT))
                for i in range(HEADS + P_LAG):
                    if i < HEADS:
                        h = i
                        blk, half = h // 2, h % 2
                        if h >= 2:
                            pe.wait_ge(a_exp, at(b, HEADS, h - 1))
                        for st in range(NT):
                            ins = nc.tensor.matmul(bS[half][:, st * S:(st + 1) * S],
                                                   qT[64 * half:64 * half + 64, blk * S + st * P:blk * S + (st + 1) * P],
                                                   kT[64 * half:64 * half + 64, (blk // 2) * S:(blk // 2 + 1) * S],
                                                   start=True, stop=True)
                        ins.then_inc(a_score, 1)
                    if S_LAG <= i < HEADS + S_LAG:
                        h = i - S_LAG
                        pe.wait_ge(a_exp, at(b, HEADS, h + 1))
                        if h >= 1:
                            pe.wait_ge(a_pT, at(b, HEADS, h))
                        for tc in range(NT):
                            for st in range(NT):
                                tr(bPT[:, (tc * NT + st) * P:(tc * NT + st + 1) * P],
                                   pr[h % 2][:, st * S + tc * P:st * S + (tc + 1) * P], a_pps, tc == NT - 1 and st == NT - 1)
                    if i >= P_LAG:
                        h = i - P_LAG
                        first, last = h % 8 == 0, h % 8 == 7
                        pe.wait_ge(a_pT, at(b, HEADS, h + 1))
                        if h == HEADS - 1:
                            pe.wait_ge(a_rrec, at(b, 2, 2))
                            for u in range(2):
                                for t in range(NT):
                                    tr(bPT[:, (u * NT + t) * P:(u * NT + t + 1) * P],
                                       pr[0][:, t * D + u * P:t * D + (u + 1) * P], a_rT, u == 1 and t == NT - 1)
                        dst = bC[:, (h // 8) * S:(h // 8 + 1) * S]
                        for tc in range(NT):
                            a = tc * ZCOLS + zwindow(head_of(h))
                            ins = nc.tensor.matmul(dst, z[:, a:a + P], pT[h % 2][:, tc * S:(tc + 1) * S],
                                                   start=first and tc == 0, stop=last and tc == NT - 1)
                        ins.then_inc(a_pv, 1)
                    yield
                yield
                yield
                pe.wait_ge(a_clo, at(b, 1, 1))
                for t in range(NT):
                    def cT(buf):
                        return lambda k: buf[:, k * S + t * P:k * S + (t + 1) * P]
                    exact(bS[t][:, 0:D], cT(cT_hi), cT(cT_lo), O_WO, D, 0, D, KD).then_inc(a_wo, 1)
                yield
                yield
                if not isinstance(b, int):
                    pe.wait_ge(b_hid, at(b - 1, NG, NG))
                    pe.wait_ge(b_tlo, at(b - 1, NQ, NQ - 1))
                for t in range(NT):
                    normed_T(b, 0, t, t)
                yield

            tb_left = []

            def hT_b(b, k, src, ready, n_ready):
                t = k % NT
                pe.wait_ge(ready, n_ready)
                if t == 0 and k > 0:
                    pe.wait_ge(*tb_left)
                for j in range(KD):
                    tr(hT_bank(k)[:, j * P:(j + 1) * P], src[:, j * P:(j + 1) * P], b_hps, j == KD - 1)
                if t == 0 and k > 0:
                    tb_left[:] = [b_hlo, at(b, NT_B, k + 1)]

            def normed_T(b, n, t, k):
                hT_b(b, k, hB_t[:, t, :], b_h_r, at(b, NLN * NT, n * NT + t + 1))

            def down_T(b, m, q, n_hid, need, first=0):
                pe.wait_ge(b_hid, need)
                if 0 < m < NQ - 1:
                    pe.wait_ge(*tb_left)
                tb_left[:] = [b_tlo, at(b, NQ, m + 1)]
                cs = chunks_of(n_hid, q)
                for i, (c, rows) in enumerate(cs):
                    tr(set_bank(m)[0:rows, i * P:(i + 1) * P], hid[:, first + c * P:first + c * P + rows], b_tps, i == len(cs) - 1)

            def down_mm(b, m, q, n_hid, ternary):
                cs = chunks_of(n_hid, q)
                n_c = -(-n_hid // P)
                pe.wait_ge(b_tlo, at(b, NQ, m + 1))
                for i, (c, rows) in enumerate(cs):
                    hi = hdT_hi[m % 2][0:rows, i * P:(i + 1) * P]
                    lo = hdT_lo[m % 2][0:rows, i * P:(i + 1) * P]
                    y = bY[:, 0:D]
                    if ternary:
                        w = w3q[0:rows, c * D:(c + 1) * D]
                        nc.tensor.matmul(y, hi, w, start=c == 0, stop=False)
                        ins = nc.tensor.matmul(y, lo, w, start=False, stop=c == n_c - 1)
                    else:
                        wh, wl = (p[0:rows, O_W2 + c * D:O_W2 + (c + 1) * D] for p in (w_hi, w_lo))
                        nc.tensor.matmul(y, hi, wh, start=c == 0, stop=False)
                        nc.tensor.matmul(y, hi, wl, start=False, stop=False)
                        ins = nc.tensor.matmul(y, lo, wh, start=False, stop=c == n_c - 1)
                ins.then_inc(b_down, 1)

            def mlp(b, n_hid, slots, g0, q0, ternary):
                n, nq = n_hid // INTER, -(-(-(-n_hid // P)) // 4)
                for s in range(slots):
                    if s == 1:
                        pe.wait_ge(b_hlo, at(b, NT_B, 8 if ternary else 2))
                    if s < NT * n:
                        t, gi = s // n, s % n
                        if s >= 2:
                            if ternary:
                                pe.wait_ge(b_hid, at(b, NG, g0 + s - 1))
                            else:
                                pe.wait_ge(b_silu, at(b, NM, s - 1))
                        dst = bG[s % 2]
                        if ternary:
                            for k in range(KD):
                                w = w12q[:, (k * FGROUPS + gi) * PAIR:(k * FGROUPS + gi + 1) * PAIR]
                                nc.tensor.matmul(dst[:, 0:PAIR], hT(bhT_hi, t)(k), w, start=k == 0, stop=False)
                                ins = nc.tensor.matmul(dst[:, 0:PAIR], hT(bhT_lo, t)(k), w, start=False, stop=k == KD - 1)
                        else:
                            a = group_start(gi)
                            w = PAIR + (EXPERTS if gi == 0 else 0)
                            ins = exact(dst[:, 0:w], hT(bhT_hi, t), hT(bhT_lo, t), O_W13, W13, a, a + w, KD)
                        ins.then_inc(b_grp, 1)
                    if not ternary and s == slots - 1:
                        project_b(b, 0)
                    for t, q in sets_at(n_hid, s, FW_LAG if ternary else W_LAG):
                        if q == 0 and t > 0:
                            pe.wait_ge(b_fin if ternary else b_res1, at(b, NT, t))
                        down_mm(b, q0 + t * nq + q, q, n_hid, ternary)
                    for t, q in sets_at(n_hid, s, FT_LAG if ternary else T_LAG):
                        down_T(b, q0 + t * nq + q, q, n_hid, at(b, NG, g0 + t * n + groups_for(n_hid, q)),
                               t * n_hid if ternary else 0)
                    if not ternary and s == LN1_EARLY + 2:
                        normed_T(b, 1, 0, 2)
                    yield

            def project_b(b, t):
                pe.wait_ge(b_hlo, at(b, NT_B, 3 + t))
                if t == 0:
                    pe.wait_ge(b_silu, at(b, NM, NM))
                else:
                    pe.wait_ge(b_qkvev, at(b, NT, t))
                exact(bG[0][:, :], hT(bhT_hi, t), hT(bhT_lo, t), O_WIN, 3 * D, 0, 2 * D, KD)
                exact(bG[1][:, 0:D], hT(bhT_hi, t), hT(bhT_lo, t), O_WIN, 3 * D, 2 * D, 3 * D, KD).then_inc(b_qkv, 1)

            def key_sum(b, t):
                pe.wait_ge(b_kv, at(b, NT, t + 1))
                return nc.tensor.matmul(bY[:, 0:D], ones[:, :], kv[:, t], start=t == 0, stop=t == NT - 1)

            def stream_b(b):
                pe.wait_ge(b_hlo, at(b, NT_B, 1))
                yield from mlp(b, HID, MLP_SLOTS, 0, 0, False)
                yield
                pe.wait_ge(b_qkvev, at(b, NT, 1))
                normed_T(b, 1, 1, 3)
                yield
                project_b(b, 1)
                yield
                yield
                key_sum(b, 0)
                key_sum(b, 1).then_inc(b_A, 1)
                yield
                for t in range(NT):
                    hT_b(b, 4 + t, qk_all[:, t, 0, :], b_y, at(b, NT, t + 1))
                yield
                for t in range(NT):
                    pe.wait_ge(b_hlo, at(b, NT_B, 5 + t))
                    exact((bY, bG[0])[t][:, 0:D], hT(bhT_hi, t), hT(bhT_lo, t), O_WOUT, D, 0, D, KD).then_inc(b_attn, 1)
                yield
                yield
                for t in range(NT):
                    normed_T(b, 2, t, 6 + t)
                yield
                pe.wait_ge(b_hlo, at(b, NT_B, 7))
                yield from mlp(b, FFN_HID, FFN_SLOTS, NM, NT * TQ, True)

            pe.wait_ge(ident_in, 16)
            program(pe, prepare, stream_a, stream_b)


def a_schedule(n_b, n_a):
    behind = [int(c) for c in SCHED]
    assert len(behind) == n_b and sum(behind) == n_a, (len(behind), n_b, sum(behind), n_a)
    return behind


def fold(w):
    rows, cols = w.shape
    n = -(-rows // P)
    full = np.zeros((n * P, cols), w.dtype)
    full[:rows] = w
    return full.reshape(n, P, cols).transpose(1, 0, 2).reshape(P, n * cols)


def pack_weights(i):
    wq = i["L0_attn_W_Q"].T.reshape(D, DH, 4, 2, G).transpose(0, 2, 4, 3, 1).reshape(D, D)
    wk = i["L0_attn_W_K"].T.reshape(D, DH, KV).transpose(0, 2, 1).reshape(D, P)
    wv = i["L0_attn_W_V"].T.reshape(D, DH, KV).transpose(0, 2, 1).reshape(D, P)
    cols = []
    for s in range(SHARED):
        r = slice(s * INTER, (s + 1) * INTER)
        cols += [i["L0_ffn_sw1"][r].T, i["L0_ffn_sw3"][r].T]
        if s == 0:
            cols.append(i["L0_ffn_gate_w"].T)
    for e in range(EXPERTS):
        cols += [i["L0_ffn_W1"][e], i["L0_ffn_W3"][e]]
    w2 = np.concatenate([i["L0_ffn_sw2"].T, i["L0_ffn_W2"].reshape(EXPERTS * INTER, D)], 0)
    order = channel_order()
    win = i["L1_attn_W_in"].reshape(3, D, D)[:, order, :].reshape(3 * D, D).T
    wout = i["L1_attn_W_out"].T[order]
    return np.ascontiguousarray(np.concatenate(
        [fold(np.concatenate([wq, wk, wv], 1)), fold(i["L0_attn_W_O"].T), fold(np.concatenate(cols, 1)), fold(w2),
         fold(win), fold(wout)], 1))


def channel_order():
    return np.concatenate([np.arange(0, D // 2, 2), np.arange(1, D // 2, 2), np.arange(D // 2, D)])


def rope_tables():
    f = np.float32
    pos = np.arange(S, dtype=f).reshape(NT, P)
    inv0 = f(1.0) / f(10000.0) ** (np.arange(0, DH // 2, dtype=f) * f(2.0) / f(DH))
    ang0 = pos[:, :, None] * inv0
    scale = np.concatenate([np.full(HEADS, 1.0 / np.sqrt(D)), np.ones(KV)]).astype(f)
    r0 = np.stack([np.cos(ang0), np.sin(ang0)])[:, :, :, None, :] * scale[:, None]
    rot = D // 2
    inv1 = f(1.0) / f(10000.0) ** (np.arange(0, rot, 2, dtype=f) / f(rot))
    ang1 = pos[:, :, None] * inv1
    r1 = np.stack([np.cos(ang1), np.sin(ang1)])
    return (np.ascontiguousarray(r0.transpose(2, 0, 1, 3, 4).reshape(P, -1).astype(f)),
            np.ascontiguousarray(r1.transpose(2, 0, 1, 3).reshape(P, -1).astype(f)))


def kernel(**inputs):
    import concourse.bacc as _bacc
    from concourse.bass_utils import run_bass_kernel_spmd as _run

    i = {k: np.asarray(v) for k, v in inputs.items()}
    r0, r1 = rope_tables()
    order = channel_order()
    arrays = {
        "x": np.ascontiguousarray(i["L0_attn_x"]),
        "wpack": pack_weights(i),
        "tern12": np.ascontiguousarray(np.stack(
            [fold(i[n].T).reshape(P, KD * FGROUPS, INTER) for n in ("L1_ffn_w1", "L1_ffn_w2")], 2).reshape(P, 2 * TW)),
        "tern3": np.ascontiguousarray(fold(i["L1_ffn_w3"].T)),
        "rbias": np.ascontiguousarray(i["L0_ffn_router_bias"]),
        "b_in": np.ascontiguousarray(i["L1_attn_b_in"].reshape(3, D)[:, order].reshape(-1)),
        "b_out": np.ascontiguousarray(i["L1_attn_b_out"]),
        "rope0": r0,
        "rope1": r1,
        "eye": np.eye(P, dtype=np.float32),
    }
    nc = _bacc.Bacc("TRN2", target_bir_lowering=False, num_devices=1)
    args = [nc.dram_tensor(f"in_{n}", a.shape, mybir.dt.from_np(a.dtype), kind="ExternalInput").ap()
            for n, a in arrays.items()]
    out = nc.dram_tensor("out_y", (BATCHES, S, D), F32, kind="ExternalOutput").ap()
    build(nc, *args, out)
    r = _run(nc, [{f"in_{n}": a for n, a in arrays.items()}], core_ids=[0])
    return r.results[0]["out_y"]
```
